# Optimizing a Trainium2 kernel written in Bass

```python
import numpy as np
import jax
import jax.numpy as jnp

def _softmax(x, axis=-1):
    return jax.nn.softmax(x, axis=axis)

def _gelu(x):
    return jax.nn.gelu(x, approximate=True)

def _silu(x):
    return jax.nn.silu(x)

def _sigmoid(x):
    return jax.nn.sigmoid(x)

def _layernorm(x, axis=-1, eps=1e-05):
    m = jnp.mean(x, axis=axis, keepdims=True)
    v = jnp.var(x, axis=axis, keepdims=True)
    return (x - m) / jnp.sqrt(v + eps)

def _scatter_add(tgt, idx, src, axis=0):
    return tgt.at[idx].add(src)

def _segment_sum(src, seg, n):
    return jax.ops.segment_sum(src, seg, n)
kernel_name = 'mk_vit_tower_d1_tok_img1024_r4_64fd41'

def setup_inputs(seed: int=0):
    np.random.seed(seed)
    _w = jnp.asarray

    def _rec_inputs():
        import jax
        import jax.numpy as jnp
        _rk = jax.random.key(seed)
        x = -0.00011082 + 0.999858 * jax.random.normal(jax.random.fold_in(_rk, 1), (4, 5, 128, 128), jnp.float32)
        return x
    x = _rec_inputs()

    def _L0_tok_setup():
        import jax, jax.numpy as jnp
        import numpy as np
        PATCH = 8
        EPS = 1e-05

        def _patchify(x):
            B, C, H, Wd = x.shape
            p = PATCH
            x = x.reshape(B, C, H // p, p, Wd // p, p)
            x = x.transpose(0, 2, 4, 1, 3, 5)
            return x.reshape(B, H // p * (Wd // p), C * p * p)
        key = jax.random.key(seed)
        k1, k2 = jax.random.split(key)
        B, C, H, W_ = (32, 5, 128, 128)
        in_feat, embed_dim = (C * PATCH * PATCH, 256)
        x = jax.random.normal(k1, (B, C, H, W_), dtype=jnp.float32)
        W = jax.random.normal(k2, (in_feat, embed_dim), dtype=jnp.float32) * (1.0 / np.sqrt(in_feat))
        gamma = jnp.ones((embed_dim,), dtype=jnp.float32)
        return {'x': x, 'W': W, 'gamma': gamma}
    _L0_tok_all = _L0_tok_setup()
    _L0_tok_in = {k: v for k, v in _L0_tok_all.items() if k in ('W', 'gamma')}
    del _L0_tok_all

    def _L0_attn_setup():
        import jax, jax.numpy as jnp
        import numpy as np
        D = 256
        H = 16
        DH = D // H
        key = jax.random.key(seed)
        ks = jax.random.split(key, 7)
        s = 0.02
        return {'z': jax.random.normal(ks[0], (8, 256, D), dtype=jnp.float32), 'ln_w': jnp.ones((D,), dtype=jnp.float32), 'ln_b': jnp.zeros((D,), dtype=jnp.float32), 'W_qkv': jax.random.normal(ks[1], (D, 3 * D), dtype=jnp.float32) * s, 'b_qkv': jnp.zeros((3 * D,), dtype=jnp.float32), 'W_proj': jax.random.normal(ks[2], (D, D), dtype=jnp.float32) * s, 'b_proj': jnp.zeros((D,), dtype=jnp.float32)}
    _L0_attn_all = _L0_attn_setup()
    _L0_attn_in = {k: v for k, v in _L0_attn_all.items() if k in ('ln_w', 'ln_b', 'W_qkv', 'b_qkv', 'W_proj', 'b_proj')}
    del _L0_attn_all

    def _L0_ffn_setup():
        import jax, jax.numpy as jnp
        import numpy as np
        D, H, E, K = (256, 256, 8, 2)

        def _moe(x, router_w, w_in, b_in, w_out, b_out):
            B, S, Dm = x.shape
            T = B * S
            x2 = x.reshape(T, Dm)
            logits = x2 @ router_w
            probs = jax.nn.softmax(logits, axis=-1)
            top_p, top_e = jax.lax.top_k(probs, K)
            flat_e = top_e.reshape(-1)
            flat_p = top_p.reshape(-1)
            tok = jnp.repeat(jnp.arange(T), K)
            order = jnp.argsort(flat_e)
            se, sp, st = (flat_e[order], flat_p[order], tok[order])
            xd = x2[st]
            N = xd.shape[0]
            h = jnp.zeros((N, H), x.dtype)
            for e in range(E):
                m = (se == e)[:, None]
                h = h + jnp.where(m, jax.nn.gelu(xd @ w_in[e] + b_in[e]), 0.0)
            y = jnp.zeros((N, Dm), x.dtype)
            for e in range(E):
                m = (se == e)[:, None]
                y = y + jnp.where(m, h @ w_out[e] + b_out[e], 0.0)
            y = y * sp[:, None]
            out = jnp.zeros((T, Dm), x.dtype).at[st].add(y)
            return out.reshape(B, S, Dm)
        key = jax.random.key(seed)
        ks = jax.random.split(key, 5)
        s = lambda k, shape, scale: jax.random.normal(k, shape, dtype=jnp.float32) * scale
        return {'input_batch': s(ks[0], (2, 128, D), 1.0), 'router_w': s(ks[1], (D, E), D ** (-0.5)), 'w_in': s(ks[2], (E, D, H), D ** (-0.5)), 'b_in': jnp.zeros((E, H), jnp.float32), 'w_out': s(ks[3], (E, H, D), H ** (-0.5)), 'b_out': jnp.zeros((E, D), jnp.float32)}
    _L0_ffn_all = _L0_ffn_setup()
    _L0_ffn_in = {k: v for k, v in _L0_ffn_all.items() if k in ('router_w', 'w_in', 'b_in', 'w_out', 'b_out')}
    del _L0_ffn_all
    return {'x': x, 'L0_tok_W': _L0_tok_in['W'], 'L0_tok_gamma': _L0_tok_in['gamma'], 'L0_attn_ln_w': _L0_attn_in['ln_w'], 'L0_attn_ln_b': _L0_attn_in['ln_b'], 'L0_attn_W_qkv': _L0_attn_in['W_qkv'], 'L0_attn_b_qkv': _L0_attn_in['b_qkv'], 'L0_attn_W_proj': _L0_attn_in['W_proj'], 'L0_attn_b_proj': _L0_attn_in['b_proj'], 'L0_ffn_router_w': _L0_ffn_in['router_w'], 'L0_ffn_w_in': _L0_ffn_in['w_in'], 'L0_ffn_b_in': _L0_ffn_in['b_in'], 'L0_ffn_w_out': _L0_ffn_in['w_out'], 'L0_ffn_b_out': _L0_ffn_in['b_out']}

def reference(x, L0_tok_W, L0_tok_gamma, L0_attn_ln_w, L0_attn_ln_b, L0_attn_W_qkv, L0_attn_b_qkv, L0_attn_W_proj, L0_attn_b_proj, L0_ffn_router_w, L0_ffn_w_in, L0_ffn_b_in, L0_ffn_w_out, L0_ffn_b_out):
    import jax
    import jax.numpy as jnp

    def _L0_tok_ref(x, W, gamma):
        import jax, jax.numpy as jnp
        import numpy as np
        PATCH = 8
        EPS = 1e-05

        def _patchify(x):
            B, C, H, Wd = x.shape
            p = PATCH
            x = x.reshape(B, C, H // p, p, Wd // p, p)
            x = x.transpose(0, 2, 4, 1, 3, 5)
            return x.reshape(B, H // p * (Wd // p), C * p * p)
        tokens = _patchify(x)
        h = jnp.einsum('bnf,fd->bnd', tokens, W)
        mu = jnp.mean(h, axis=-1, keepdims=True)
        var = jnp.mean(jnp.square(h - mu), axis=-1, keepdims=True)
        out = (h - mu) * jax.lax.rsqrt(var + EPS) * gamma
        return out

    def _L0_attn_ref(z, ln_w, ln_b, W_qkv, b_qkv, W_proj, b_proj):
        import jax, jax.numpy as jnp
        import numpy as np
        D = 256
        H = 16
        DH = D // H
        b, n, d = z.shape
        mu = jnp.mean(z, axis=-1, keepdims=True)
        var = jnp.var(z, axis=-1, keepdims=True)
        zn = (z - mu) / jnp.sqrt(var + 1e-05) * ln_w + ln_b
        qkv = (zn @ W_qkv + b_qkv).reshape(b, n, 3, H, DH)
        q = qkv[:, :, 0].transpose(0, 2, 1, 3)
        k = qkv[:, :, 1].transpose(0, 2, 1, 3)
        v = qkv[:, :, 2].transpose(0, 2, 1, 3)
        scale = 1.0 / jnp.sqrt(jnp.asarray(DH, dtype=z.dtype))
        scores = jnp.einsum('bhqd,bhkd->bhqk', q, k) * scale
        attn = jax.nn.softmax(scores, axis=-1)
        msa = jnp.einsum('bhqk,bhkd->bhqd', attn, v)
        msa_cat = msa.transpose(0, 2, 1, 3).reshape(b, n, d)
        out = msa_cat @ W_proj + b_proj
        return z + out

    def _L0_ffn_ref(input_batch, router_w, w_in, b_in, w_out, b_out):
        import jax, jax.numpy as jnp
        import numpy as np
        D, H, E, K = (256, 256, 8, 2)

        def _moe(x, router_w, w_in, b_in, w_out, b_out):
            B, S, Dm = x.shape
            T = B * S
            x2 = x.reshape(T, Dm)
            logits = x2 @ router_w
            probs = jax.nn.softmax(logits, axis=-1)
            top_p, top_e = jax.lax.top_k(probs, K)
            flat_e = top_e.reshape(-1)
            flat_p = top_p.reshape(-1)
            tok = jnp.repeat(jnp.arange(T), K)
            order = jnp.argsort(flat_e)
            se, sp, st = (flat_e[order], flat_p[order], tok[order])
            xd = x2[st]
            N = xd.shape[0]
            h = jnp.zeros((N, H), x.dtype)
            for e in range(E):
                m = (se == e)[:, None]
                h = h + jnp.where(m, jax.nn.gelu(xd @ w_in[e] + b_in[e]), 0.0)
            y = jnp.zeros((N, Dm), x.dtype)
            for e in range(E):
                m = (se == e)[:, None]
                y = y + jnp.where(m, h @ w_out[e] + b_out[e], 0.0)
            y = y * sp[:, None]
            out = jnp.zeros((T, Dm), x.dtype).at[st].add(y)
            return out.reshape(B, S, Dm)
        return _moe(input_batch, router_w, w_in, b_in, w_out, b_out)
    h = _L0_tok_ref(x, L0_tok_W, L0_tok_gamma)
    h = h + _L0_attn_ref(_layernorm(h, axis=-1), L0_attn_ln_w, L0_attn_ln_b, L0_attn_W_qkv, L0_attn_b_qkv, L0_attn_W_proj, L0_attn_b_proj)
    h = h + _L0_ffn_ref(_layernorm(h, axis=-1), L0_ffn_router_w, L0_ffn_w_in, L0_ffn_b_in, L0_ffn_w_out, L0_ffn_b_out)
    return h

_drawn_inputs = setup_inputs


def setup_inputs(seed=0):
    import zlib

    import numpy as np

    out = dict(_drawn_inputs(seed))
    spreads = {'L0_tok_gamma': (1.0, 0.2),
     'L0_attn_ln_w': (1.0, 0.6),
     'L0_attn_ln_b': (0.0, 0.8),
     'L0_attn_b_qkv': (0.0, 0.434),
     'L0_attn_b_proj': (0.0, 0.277),
     'L0_ffn_b_in': (0.0, 0.545),
     'L0_ffn_b_out': (0.0, 0.374)}
    factors = {'L0_attn_W_qkv': 6.793, 'L0_attn_W_proj': 3.002}
    for name, (base, spread) in spreads.items():
        noise = np.random.default_rng([zlib.crc32(name.encode()), seed]).standard_normal(out[name].shape)
        drawn = base * np.exp(spread * noise) if base else spread * noise
        out[name] = jnp.asarray(drawn.astype(out[name].dtype))
    for name, factor in factors.items():
        out[name] = (out[name] * factor).astype(out[name].dtype)
    return out
```

```python
from contextlib import ExitStack

import concourse.bass as bass
from concourse import mybir

F32 = mybir.dt.float32
F32R = mybir.dt.float32r
BF16 = mybir.dt.bfloat16
U32 = mybir.dt.uint32
ALU = mybir.AluOpType
ACT = mybir.ActivationFunctionType
AX = mybir.AxisListType.X

P = 128
B, N, D, H, DH, E = 4, 256, 256, 16, 16, 8
NT = N // P
NC = D // P
KF = 107
NF = 3
EPS = 1e-5
SCALE = DH ** -0.5
Q_PIECE = [0, 0, 1, 1, 0, 2]
K_PIECE = [0, 1, 0, 1, 2, 0]
SLOTS = len(Q_PIECE)
MROW = SLOTS * DH
KSC = MROW + 3
G = 4


def build(nc, xT, w_tok, gamma, ln_w, ln_b, w_qk, w_v, b_qk, b_v, w_proj, b_proj, w_router,
          w_in, b_in, w_out, b_out, ident_c, iota_c, out):
    with ExitStack() as ctx:
        def sb(name, shape, dt=F32):
            return ctx.enter_context(nc.sbuf_tensor(name, shape, dt))

        def sem(name):
            return ctx.enter_context(nc.semaphore(name))

        bank = [ctx.enter_context(nc.psum_tensor(f"bank{i}", [P, 512], F32)) for i in range(8)]
        ps_s, ps_t, ps_l1 = bank[0:2], bank[2:4], bank[4:6]
        ps_l2, ps_x = bank[6], bank[7]

        ident = sb("ident", [P, P])
        iota = sb("iota", [P, E])
        gam = sb("gam", [P, D])
        bv = sb("bv", [P, D])
        bp = sb("bp", [P, D])
        bo = sb("bo", [E, D])
        lnw = sb("lnw", [P, NC])
        lnb = sb("lnb", [P, NC])
        bqk = sb("bqk", [P, 4])
        bin_ = sb("bin", [P, E, NC])
        nhalf = sb("nhalf", [P, NT])
        wt_raw, wt_hi, wt_lo = sb("wt_raw", [KF, NF, D]), sb("wt_hi", [KF, NF, D], F32R), sb("wt_lo", [KF, NF, D], F32R)
        stage_a = sb("stage_a", [P, NC * (4 * P + 2 * D + E)])
        wa_raw = stage_a[:].rearrange("p (c n) -> p c n", c=NC)
        qk = stage_a[:, 0:4 * N].rearrange("p (m n) -> p m n", m=4)
        qk_r = stage_a[:, 4 * N:8 * N].rearrange("p (m n) -> p m n", m=4)
        wa_hi = sb("wa_hi", [P, NC, 4 * P + D + D + P], F32R)
        wa_lo = sb("wa_lo", [P, NC, 4 * P + D + D + P], F32R)
        OV, OP, OR = 4 * P, 4 * P + D, 4 * P + 2 * D
        stage_i = sb("stage_i", [P, E * NC * D])
        wi_raw = stage_i[:].rearrange("p (e c n) -> p e c n", e=E, c=NC)
        probs = stage_i[:].rearrange("p (h t n) -> p h t n", h=2 * G, t=NT)
        wi_hi = sb("wi_hi", [P, E, NC, D], F32R)
        wi_lo = sb("wi_lo", [P, E, NC, D], F32R)
        wo = sb("wo", [P, E, NC, D])

        x_raw = sb("x_raw", [KF, NF, N])
        x_hi = sb("x_hi", [KF, NF, N], F32R)
        x_lo = sb("x_lo", [KF, NF, N], F32R)
        stats = sb("stats", [P, NT, 6])
        mv = sb("mv", [P, NT, 2])
        var_eps = sb("var_eps", [P, NT])
        rstd = sb("rstd", [P, NT])
        h0 = sb("h0", [P, NT, D])
        z = sb("z", [P, NT, D])
        zn = sb("zn", [P, NT, D])
        resid = [sb(f"resid{i}", [P, NT, D]) for i in range(2)]
        znT = sb("znT", [P, NC, N])
        znT_hi, znT_lo = sb("znT_hi", [P, NC, N], F32R), sb("znT_lo", [P, NC, N], F32R)
        piece = [sb(f"piece{i}", [P, 4, N], BF16) for i in range(3)]
        q_st = [sb(f"q_st{i}", [P, H, N], BF16) for i in range(2)]
        k_st = [sb(f"k_st{i}", [P, H, N], BF16) for i in range(2)]
        v_aug = [sb(f"v_aug{i}", [P, NT, H, 2 * DH]) for i in range(2)]
        neg_max = sb("neg_max", [P, NT, H])
        m_row = sb("m_row", [H // 2, 3, N], BF16)
        m_rem = sb("m_rem", [H // 2, N])
        oT = sb("oT", [P, G, N])
        o_rs = sb("o_rs", [P, NT, H])
        o_n = sb("o_n", [P, NT, D])
        oT_hi, oT_lo = sb("oT_hi", [P, NC, N], F32R), sb("oT_lo", [P, NC, N], F32R)
        h1 = sb("h1", [P, NT, D])
        x2 = sb("x2", [P, NT, D])
        x2T_hi, x2T_lo = sb("x2T_hi", [P, NC, N], F32R), sb("x2T_lo", [P, NC, N], F32R)
        lgT = sb("lgT", [E, N])
        lg_max = sb("lg_max", [P, NT])
        ex = sb("ex", [P, NT, E])
        ex_sum = sb("ex_sum", [P, NT])
        ex_rs = sb("ex_rs", [P, NT])
        pr = sb("pr", [P, NT, E])
        top_p = sb("top_p", [P, NT, 8])
        top_i = sb("top_i", [P, NT, 8], U32)
        top_f = sb("top_f", [P, NT, 8])
        gate_a, gate_b, gate = sb("gate_a", [P, NT, E]), sb("gate_b", [P, NT, E]), sb("gate", [P, NT, E])
        gateT = sb("gateT", [E, N])
        acc = [sb(f"acc{i}", [P, NT, D]) for i in range(2)]
        g = [sb(f"g{i}", [P, NC, N]) for i in range(2)]

        d_x = sem("d_x")
        d_wt, d_wa, d_wi, d_wo, d_c, d_out = sem("d_wt"), sem("d_wa"), sem("d_wi"), sem("d_wo"), sem("d_c"), sem("d_out")
        d_stack = [sem(f"d_stack{i}") for i in range(2)]
        d_m = [sem(f"d_m{i}") for i in range(2)]
        dve_own, s_xlo, s_wt, s_wa, s_wihi = sem("dve_own"), sem("s_xlo"), sem("s_wt"), sem("s_wa"), sem("s_wihi")
        s_mv, s_zn, s_vaug, s_max, s_mrow = sem("s_mv"), sem("s_zn"), sem("s_vaug"), sem("s_max"), sem("s_mrow")
        s_resid, s_on, s_otlo, s_x2, s_x2lo = sem("s_resid"), sem("s_on"), sem("s_otlo"), sem("s_x2"), sem("s_x2lo")
        s_lgmax, s_gate, s_gateT, s_accini, s_acc = sem("s_lgmax"), sem("s_gate"), sem("s_gateT"), sem("s_accini"), sem("s_acc")
        s_ones = sem("s_ones")
        s_tok, s_znTp, s_qkp, s_vp = sem("s_tok"), sem("s_znTp"), sem("s_qkp"), sem("s_vp")
        s_S, s_mT, s_ST, s_pv = sem("s_S"), sem("s_mT"), sem("s_ST"), sem("s_pv")
        s_oTp, s_onTp, s_proj, s_x2Tp = sem("s_oTp"), sem("s_onTp"), sem("s_proj"), sem("s_x2Tp")
        s_lgTp, s_lgp, s_gTp, s_bo = sem("s_lgTp"), sem("s_lgp"), sem("s_gTp"), sem("s_bo")
        s_l1, s_l2 = sem("s_l1"), sem("s_l2")
        s_znT, s_p1, s_qkf, s_exp = sem("s_znT"), sem("s_p1"), sem("s_qkf"), sem("s_exp")
        s_oT, s_othi, s_x2hi, s_lgT, s_ex, s_gelu = sem("s_oT"), sem("s_othi"), sem("s_x2hi"), sem("s_lgT"), sem("s_ex"), sem("s_gelu")
        pool_own, s_rstd, s_znhi, s_znlo, s_pieces, s_wilo, s_nhalf = (
            sem("pool_own"), sem("s_rstd"), sem("s_znhi"), sem("s_znlo"), sem("s_pieces"), sem("s_wilo"), sem("s_nhalf"))

        CONSTS = 10
        out_v = out.rearrange("b (t p) d -> b p t d", p=P)

        def half(bk, i):
            return bk[:, i * N:(i + 1) * N]

        def both(bk):
            return bk[:, :].rearrange("p (t n) -> p t n", n=N)

        block = ctx.enter_context(nc.Block())

        @block.sync
        def _(sp):
            def load_x(b):
                if b >= 1:
                    sp.wait_ge(s_xlo, b)
                sp.dma_start(x_raw[:], xT[:, :, b * N:(b + 1) * N]).then_inc(d_x, 16)

            def stack(b):
                sp.wait_ge(s_pieces, b + 1)
                if b >= 2:
                    sp.wait_ge(s_ST, H * (b - 1))
                for st, half0, table in ((q_st[b % 2], 0, Q_PIECE), (k_st[b % 2], 2, K_PIECE)):
                    for s, pc in enumerate(table):
                        src = piece[pc][:, half0:half0 + 2, :]
                        dst = st[s * DH:(s + 1) * DH, :, :].rearrange("d (h m) n -> d h (m n)", m=2)
                        sp.dma_start(dst, src).then_inc(d_stack[b % 2], 16)

            def max_rows(b, hh):
                sp.wait_ge(s_mrow, 2 * b + hh + 1)
                for r in range(3):
                    sp.dma_start(q_st[b % 2][MROW + r:MROW + r + 1, hh * 8:hh * 8 + 8, :],
                                 m_row[:, r, :]).then_inc(d_m[hh], 16)

            sp.dma_start(wt_raw[:], w_tok).then_inc(d_wt, 16)
            load_x(0)
            sp.dma_start(wa_raw[:, :, 0:OV], w_qk).then_inc(d_wa, 16)
            sp.dma_start(wa_raw[:, :, OV:OP], w_v).then_inc(d_wa, 16)
            sp.dma_start(wa_raw[:, :, OP:OR], w_proj).then_inc(d_wa, 16)
            sp.dma_start(wa_raw[:, :, OR:OR + E], w_router).then_inc(d_wa, 16)
            sp.dma_start(wi_raw, w_in).then_inc(d_wi, 16)
            sp.dma_start(wo[:], w_out).then_inc(d_wo, 16)
            load_x(1)
            stack(0)
            for t in range(B):
                for hh in range(2):
                    max_rows(t, hh)
                if t >= 1:
                    sp.wait_ge(s_acc, NT * E * t)
                    sp.dma_start(out_v[t - 1], acc[(t - 1) % 2][:]).then_inc(d_out, 16)
                if t + 1 < B:
                    if t + 2 < B:
                        load_x(t + 2)
                    stack(t + 1)
            sp.wait_ge(s_acc, NT * E * B)
            sp.dma_start(out_v[B - 1], acc[(B - 1) % 2][:]).then_inc(d_out, 16)
            sp.wait_ge(d_out, 16 * B)

        @block.gpsimd
        def _(pool):
            n_own = [0]

            def link(ins):
                n_own[0] += 1
                ins.then_inc(pool_own, 1)
                pool.wait_ge(pool_own, n_own[0])

            def rsqrt(k):
                pool.wait_ge(s_mv, k + 1)
                link(pool.tensor_scalar(var_eps[:], mv[:, :, 1], EPS, None, ALU.add))
                pool.tensor_tensor(rstd[:], var_eps[:], nhalf[:], ALU.pow).then_inc(s_rstd, 1)

            def front(b):
                for i in range(3):
                    rsqrt(ln_index(b, i))
                pool.wait_ge(s_znhi, b + 1)
                pool.wait_ge(s_znT, b + 1)
                if b >= 1:
                    pool.wait_ge(s_vp, b)
                pool.tensor_tensor(znT_lo[:], znT[:], znT_hi[:].bitcast(F32), ALU.subtract).then_inc(s_znlo, 1)
                pool.wait_ge(s_p1, b + 1)
                pool.wait_ge(s_qkf, b + 1)
                link(pool.tensor_tensor(qk_r, qk, piece[0][:], ALU.subtract))
                if b >= 1:
                    pool.wait_ge(d_stack[(b - 1) % 2], 16 * 2 * SLOTS * ((b - 1) // 2 + 1))
                link(pool.tensor_copy(piece[1][:], qk_r))
                pool.tensor_tensor(piece[2][:], qk_r, piece[1][:], ALU.subtract).then_inc(s_pieces, 1)

            pool.memset(nhalf[:], -0.5).then_inc(s_nhalf, 1)
            pool.wait_ge(s_nhalf, 1)
            for i in range(2):
                pool.memset(v_aug[i][:, :, :, DH:2 * DH], 1.0).then_inc(s_ones, 1)
                pool.wait_ge(s_ones, 2 * i + 1)
                pool.memset(k_st[i][MROW:KSC, :, :], 1.0).then_inc(s_ones, 1)
                pool.wait_ge(s_ones, 2 * i + 2)
            front(0)
            pool.wait_ge(s_wihi, 1)
            pool.tensor_tensor(wi_lo[:], wi_raw, wi_hi[:].bitcast(F32), ALU.subtract).then_inc(s_wilo, 1)
            for t in range(B):
                if t + 1 < B:
                    front(t + 1)
                rsqrt(ln_index(t, 3))

        @block.scalar
        def _(act):
            act.dma_start(ident[:], ident_c).then_inc(d_c, 16)
            act.dma_start(iota[:], iota_c).then_inc(d_c, 16)
            act.dma_start(gam[:], gamma.partition_broadcast(P)).then_inc(d_c, 16)
            act.dma_start(lnw[:], ln_w).then_inc(d_c, 16)
            act.dma_start(lnb[:], ln_b).then_inc(d_c, 16)
            act.dma_start(bqk[:], b_qk).then_inc(d_c, 16)
            act.dma_start(bv[:], b_v.partition_broadcast(P)).then_inc(d_c, 16)
            act.dma_start(bp[:], b_proj.partition_broadcast(P)).then_inc(d_c, 16)
            act.dma_start(bo[:], b_out).then_inc(d_c, 16)
            act.dma_start(bin_[:], b_in).then_inc(d_c, 16)

            def znT_out(b):
                act.wait_ge(s_znTp, b + 1)
                if b == 0:
                    act.wait_ge(d_c, 16 * CONSTS)
                if b >= 1:
                    act.wait_ge(s_znlo, b)
                act.activation(znT[:, 0, :], half(ps_l1[1], 0), ACT.Identity, bias=lnb[:, 0:1], scale=lnw[:, 0:1])
                act.activation(znT[:, 1, :], half(ps_l1[1], 1), ACT.Identity, bias=lnb[:, 1:2],
                               scale=lnw[:, 1:2]).then_inc(s_znT, 1)

            def qk_out(b):
                act.wait_ge(s_qkp, b + 1)
                if b >= 1:
                    act.wait_ge(s_pieces, b)
                    act.wait_ge(d_stack[(b - 1) % 2], 16 * 2 * SLOTS * ((b - 1) // 2 + 1))
                for m in range(4):
                    src = half((ps_l2, ps_x)[m // 2], m % 2)
                    i1 = act.activation(piece[0][:, m, :], src, ACT.Identity, bias=bqk[:, m:m + 1])
                    if m == 3:
                        i1.then_inc(s_p1, 1)
                    i2 = act.activation(qk[:, m, :], src, ACT.Identity, bias=bqk[:, m:m + 1])
                    if m == 3:
                        i2.then_inc(s_qkf, 1)

            def exp(b, h):
                act.wait_ge(s_ST, H * b + h + 1)
                if b == 0 and h == 0:
                    act.wait_ge(s_wilo, 1)
                if H * b + h >= 2 * G:
                    act.wait_ge(s_pv, (H * b + h - 2 * G) // G + 1)
                act.activation(probs[:, h % (2 * G), :, :], both(ps_t[h % 2]), ACT.Exp, scale=SCALE).then_inc(s_exp, 1)

            def post(b):
                act.wait_ge(s_pv, G * (b + 1))
                if b >= 1:
                    act.wait_ge(s_oTp, b)
                for i in range(2):
                    last = act.activation(oT[:, 2 * i:2 * i + 2, :], both(ps_s[i]), ACT.Copy)
                last.then_inc(s_oT, 1)
                act.wait_ge(s_onTp, b + 1)
                if b >= 1:
                    act.wait_ge(s_proj, b)
                act.activation(oT_hi[:], both(ps_s[0]), ACT.Copy).then_inc(s_othi, 1)
                act.wait_ge(s_x2Tp, b + 1)
                if b >= 1:
                    act.wait_ge(s_l1, E * b)
                act.activation(x2T_hi[:], both(ps_t[0]), ACT.Copy).then_inc(s_x2hi, 1)
                act.wait_ge(s_lgTp, b + 1)
                if b >= 1:
                    act.wait_ge(s_lgp, b)
                act.activation(lgT[:], ps_t[1][0:E, 0:N], ACT.Copy).then_inc(s_lgT, 1)
                act.wait_ge(s_lgmax, b + 1)
                for tt in range(NT):
                    last = act.activation(ex[:, tt, :], ps_s[0][:, tt * E:(tt + 1) * E], ACT.Exp, bias=lg_max[:, tt:tt + 1])
                last.then_inc(s_ex, 1)

            def gelu(b, e):
                k = E * b + e
                act.wait_ge(s_l1, k + 1)
                if k >= 2:
                    act.wait_ge(s_l2, k - 1)
                for hc in range(NC):
                    last = act.activation(g[e % 2][:, hc, :], half(ps_l1[e % 2], hc), ACT.Gelu_apprx_tanh,
                                          bias=bin_[:, e, hc:hc + 1])
                last.then_inc(s_gelu, 1)

            znT_out(0)
            qk_out(0)
            for t in range(B + 1):
                if t >= 1:
                    for e in range(E):
                        gelu(t - 1, e)
                if t == B:
                    break
                for h in range(H):
                    exp(t, h)
                    if h == 7 and t + 1 < B:
                        znT_out(t + 1)
                    if h == 11 and t + 1 < B:
                        qk_out(t + 1)
                post(t)

        @block.vector
        def _(dve):
            n_own = [0]

            def link(ins):
                n_own[0] += 1
                ins.then_inc(dve_own, 1)
                dve.wait_ge(dve_own, n_own[0])

            def moments(src, k):
                for tt in range(NT):
                    ins = dve.bn_stats(stats[:, tt, :], src[:, tt, :])
                link(ins)
                if k >= 1:
                    dve.wait_ge(s_rstd, k)
                for tt in range(NT):
                    ins = dve.bn_aggr(mv[:, tt, :], stats[:, tt, :])
                ins.then_inc(s_mv, 1)
                dve.wait_ge(s_rstd, k + 1)

            def normed(dst, src, done=None):
                for tt in range(NT):
                    ins = dve.tensor_scalar(dst[:, tt, :], src[:, tt, :], mv[:, tt, 0:1], rstd[:, tt:tt + 1],
                                            ALU.subtract, ALU.mult)
                if done is None:
                    link(ins)
                else:
                    ins.then_inc(done, 1)

            def split_x(b):
                dve.wait_ge(d_x, 16 * (b + 1))
                if b >= 1:
                    dve.wait_ge(s_tok, b)
                link(dve.tensor_copy(x_hi[:], x_raw[:]))
                dve.tensor_tensor(x_lo[:], x_raw[:], x_hi[:].bitcast(F32), ALU.subtract).then_inc(s_xlo, 1)

            def norms(b):
                dve.wait_ge(s_tok, b + 1)
                tok = both(ps_l1[0])
                moments(tok, ln_index(b, 0))
                normed(z, tok)
                if b == 0:
                    dve.wait_ge(d_c, 16 * CONSTS)
                for tt in range(NT):
                    ins = dve.tensor_tensor(h0[:, tt, :], z[:, tt, :], gam[:], ALU.mult)
                link(ins)
                moments(h0, ln_index(b, 1))
                normed(z, h0)
                moments(z, ln_index(b, 2))
                if b >= 1:
                    dve.wait_ge(s_znTp, b)
                normed(zn, z, s_zn)

            def front_rest(b):
                dve.wait_ge(s_zn, b + 1)
                link(dve.tensor_tensor(z[:], z[:], h0[:], ALU.add))
                for tt in range(NT):
                    ins = dve.tensor_tensor(resid[b % 2][:, tt, :], z[:, tt, :], bp[:], ALU.add)
                ins.then_inc(s_resid, 1)
                dve.wait_ge(s_resid, b + 1)
                dve.wait_ge(s_znT, b + 1)
                if b >= 1:
                    dve.wait_ge(s_vp, b)
                dve.tensor_copy(znT_hi[:], znT[:]).then_inc(s_znhi, 1)
                dve.wait_ge(s_vp, b + 1)
                if b == 0:
                    dve.wait_ge(s_ones, 4)
                if b >= 2:
                    dve.wait_ge(s_pv, G * (b - 1))
                for tt in range(NT):
                    ins = dve.tensor_tensor(v_aug[b % 2][:, tt, :, 0:DH],
                                            half(ps_l1[0], tt).rearrange("p (h d) -> p h d", d=DH),
                                            bv[:].rearrange("p (h d) -> p h d", d=DH), ALU.add)
                ins.then_inc(s_vaug, 1)

            def head_max(b, h):
                dve.wait_ge(s_S, H * b + h + 1)
                if h == 0 and b >= 1:
                    dve.wait_ge(s_mT, 2 * b)
                dve.tensor_reduce(neg_max[:, :, h], both(ps_s[h % 2]), AX, ALU.max, negate=True).then_inc(s_max, 1)

            def max_pieces(b, hh):
                k = 2 * b + hh
                dve.wait_ge(s_mT, k + 1)
                if k >= 1:
                    dve.wait_ge(d_m[(k - 1) % 2], 48 * ((k - 1) // 2 + 1))
                src = ps_x[0:H // 2, 0:N]
                link(dve.tensor_copy(m_row[:, 0, :], src))
                link(dve.tensor_tensor(m_rem[:], src, m_row[:, 0, :], ALU.subtract))
                link(dve.tensor_copy(m_row[:, 1, :], m_rem[:]))
                dve.tensor_tensor(m_row[:, 2, :], m_rem[:], m_row[:, 1, :], ALU.subtract).then_inc(s_mrow, 1)

            def add_expert(b, e):
                k = E * b + e
                dve.wait_ge(s_l2, k + 1)
                a = acc[b % 2]
                if e >= 1:
                    dve.wait_ge(s_acc, NT * k)
                for tt in range(NT):
                    dve.scalar_tensor_tensor(out=a[:, tt, :], in0=half(ps_l2, tt), scalar=gate[:, tt, e:e + 1],
                                             in1=a[:, tt, :], op0=ALU.mult, op1=ALU.add).then_inc(s_acc, 1)

            def post(b):
                dve.wait_ge(s_oTp, b + 1)
                heads = [ps_t[tt][:, :].rearrange("p (h d) -> p h d", d=2 * DH) for tt in range(NT)]
                for tt in range(NT):
                    ins = dve.reciprocal(o_rs[:, tt, :], heads[tt][:, :, DH])
                link(ins)
                for tt in range(NT):
                    ins = dve.tensor_tensor(o_n[:, tt, :].rearrange("p (h d) -> p h d", d=DH), heads[tt][:, :, 0:DH],
                                            o_rs[:, tt, :].unsqueeze(2).to_broadcast([P, H, DH]), ALU.mult)
                ins.then_inc(s_on, 1)
                dve.wait_ge(s_othi, b + 1)
                dve.tensor_tensor(oT_lo[:], both(ps_s[0]), oT_hi[:].bitcast(F32), ALU.subtract).then_inc(s_otlo, 1)
                dve.wait_ge(s_proj, b + 1)
                link(dve.tensor_tensor(h1[:], both(ps_s[1]), resid[b % 2][:], ALU.add))
                moments(h1, ln_index(b, 3))
                normed(x2, h1, s_x2)
                dve.wait_ge(s_x2hi, b + 1)
                dve.tensor_tensor(x2T_lo[:], both(ps_t[0]), x2T_hi[:].bitcast(F32), ALU.subtract).then_inc(s_x2lo, 1)
                dve.wait_ge(s_lgp, b + 1)
                lg = ps_s[0][:, 0:NT * E].rearrange("p (t e) -> p t e", e=E)
                dve.tensor_reduce(lg_max[:], lg, AX, ALU.max, negate=True).then_inc(s_lgmax, 1)
                dve.wait_ge(s_ex, b + 1)
                link(dve.tensor_reduce(ex_sum[:], ex[:], AX, ALU.add))
                link(dve.reciprocal(ex_rs[:], ex_sum[:]))
                link(dve.tensor_tensor(pr[:], ex[:], ex_rs[:].unsqueeze(2).to_broadcast([P, NT, E]), ALU.mult))
                for tt in range(NT):
                    link(dve.max(top_p[:, tt, :], pr[:, tt, :]))
                    link(dve.max_index(top_i[:, tt, :], top_p[:, tt, :], pr[:, tt, :]))
                link(dve.tensor_copy(top_f[:], top_i[:]))
                for tt in range(NT):
                    for i, dst in enumerate((gate_a, gate_b)):
                        ins = dve.tensor_scalar(dst[:, tt, :], iota[:], top_f[:, tt, i:i + 1], top_p[:, tt, i:i + 1],
                                                ALU.is_equal, ALU.mult)
                link(ins)
                dve.tensor_tensor(gate[:], gate_a[:], gate_b[:], ALU.add).then_inc(s_gate, 1)
                dve.wait_ge(s_gTp, b + 1)
                dve.tensor_copy(gateT[:], ps_t[1][0:E, 0:N]).then_inc(s_gateT, 1)
                dve.wait_ge(s_bo, b + 1)
                if b >= 2:
                    dve.wait_ge(d_out, 16 * (b - 1))
                dve.tensor_tensor(acc[b % 2][:], both(ps_s[1]), h1[:], ALU.add).then_inc(s_accini, 1)
                dve.wait_ge(s_accini, b + 1)

            dve.wait_ge(d_wt, 16)
            link(dve.tensor_copy(wt_hi[:], wt_raw[:]))
            dve.tensor_tensor(wt_lo[:], wt_raw[:], wt_hi[:].bitcast(F32), ALU.subtract).then_inc(s_wt, 1)
            split_x(0)
            dve.wait_ge(d_wa, 64)
            link(dve.memset(wa_hi[:, :, OR:OR + P].bitcast(F32), 0.0))
            link(dve.memset(wa_lo[:, :, OR:OR + P].bitcast(F32), 0.0))
            link(dve.tensor_copy(wa_hi[:, :, 0:OR + E], wa_raw))
            dve.tensor_tensor(wa_lo[:, :, 0:OR + E], wa_raw, wa_hi[:, :, 0:OR + E].bitcast(F32),
                              ALU.subtract).then_inc(s_wa, 1)
            norms(0)
            front_rest(0)
            dve.wait_ge(d_wi, 16)
            dve.tensor_copy(wi_hi[:], wi_raw).then_inc(s_wihi, 1)
            for t in range(B + 1):
                for e in range(E):
                    if t < B:
                        head_max(t, 2 * e)
                        head_max(t, 2 * e + 1)
                        if e == 4:
                            max_pieces(t, 0)
                    if t >= 1 and e >= 1:
                        add_expert(t - 1, e - 1)
                if t < B:
                    max_pieces(t, 1)
                if t >= 1:
                    add_expert(t - 1, E - 1)
                if t == B:
                    break
                if t + 1 < B:
                    split_x(t + 1)
                    norms(t + 1)
                    front_rest(t + 1)
                post(t)

        @block.tensor
        def _(pe):
            def product(o, pairs):
                for i, (w, x) in enumerate(pairs):
                    mm = pe.matmul(o, w, x, start=(i == 0), stop=(i == len(pairs) - 1))
                return mm

            def three(w_hi, w_lo, x_hi_, x_lo_):
                return [(w_hi, x_hi_), (w_lo, x_hi_), (w_hi, x_lo_)]

            def tok(b):
                pe.wait_ge(s_xlo, b + 1)
                if b == 0:
                    pe.wait_ge(s_wt, 1)
                if b >= 1:
                    pe.wait_ge(s_vaug, b)
                if b >= 2:
                    pe.wait_ge(s_gelu, E * (b - 1))
                for tt in range(NT):
                    c = slice(tt * P, (tt + 1) * P)
                    mm = product(half(ps_l1[0], tt), [
                        pr for f in range(NF)
                        for pr in three(x_hi[:, f, c], x_lo[:, f, c], wt_hi[:, f, :], wt_lo[:, f, :])])
                mm.then_inc(s_tok, 1)

            def zn_transposes(b):
                pe.wait_ge(s_zn, b + 1)
                if b == 0:
                    pe.wait_ge(d_c, 16 * CONSTS)
                if b >= 1:
                    pe.wait_ge(s_znT, b)
                for c in range(NC):
                    for tt in range(NT):
                        mm = pe.transpose(ps_l1[1][:, c * N + tt * P:c * N + (tt + 1) * P],
                                          zn[:, tt, c * P:(c + 1) * P], ident[:])
                mm.then_inc(s_znTp, 1)

            def qkv(b):
                pe.wait_ge(s_znhi, b + 1)
                pe.wait_ge(s_znlo, b + 1)
                if b == 0:
                    pe.wait_ge(s_wa, 1)
                if b >= 1:
                    pe.wait_ge(s_qkf, b)
                    pe.wait_ge(s_mrow, 2 * b)
                if b >= 2:
                    pe.wait_ge(s_acc, NT * E * (b - 1))
                for m in range(4):
                    cols = slice(m * P, (m + 1) * P)
                    mm = product(half((ps_l2, ps_x)[m // 2], m % 2), [
                        pr for c in range(NC)
                        for pr in three(wa_hi[:, c, cols], wa_lo[:, c, cols], znT_hi[:, c, :], znT_lo[:, c, :])])
                mm.then_inc(s_qkp, 1)
                for tt in range(NT):
                    t_ = slice(tt * P, (tt + 1) * P)
                    mm = product(half(ps_l1[0], tt), [
                        pr for c in range(NC)
                        for pr in three(znT_hi[:, c, t_], znT_lo[:, c, t_], wa_hi[:, c, OV:OP], wa_lo[:, c, OV:OP])])
                mm.then_inc(s_vp, 1)

            def scores(b, h):
                if h == 0:
                    pe.wait_ge(d_stack[b % 2], 16 * 2 * SLOTS * (b // 2 + 1))
                    if b >= 1:
                        pe.wait_ge(s_accini, b)
                if H * b + h >= 2:
                    pe.wait_ge(s_max, H * b + h - 1)
                for tt in range(NT):
                    mm = pe.matmul(half(ps_s[h % 2], tt), q_st[b % 2][0:MROW, h, tt * P:(tt + 1) * P],
                                   k_st[b % 2][0:MROW, h, :], start=True, stop=True)
                mm.then_inc(s_S, 1)

            def max_transposes(b, hh):
                pe.wait_ge(s_max, H * b + 8 * hh + 8)
                if b >= 1 or hh == 1:
                    pe.wait_ge(s_mrow, 2 * b + hh)
                pe.wait_ge(s_qkf, b + 1)
                for tt in range(NT):
                    mm = pe.transpose(ps_x[0:H // 2, tt * P:(tt + 1) * P], neg_max[:, tt, 8 * hh:8 * hh + 8], ident[:])
                mm.then_inc(s_mT, 1)

            def scores_t(b, h):
                if h % 8 == 0:
                    pe.wait_ge(d_m[h // 8], 48 * (b + 1))
                if h == 0 and b == 0:
                    pe.wait_ge(s_ones, 4)
                if h == 0 and b >= 1:
                    pe.wait_ge(s_gateT, b)
                if H * b + h >= 2:
                    pe.wait_ge(s_exp, H * b + h - 1)
                for tt in range(NT):
                    mm = pe.matmul(half(ps_t[h % 2], tt), k_st[b % 2][0:KSC, h, tt * P:(tt + 1) * P],
                                   q_st[b % 2][0:KSC, h, :], start=True, stop=True)
                mm.then_inc(s_ST, 1)

            def pv(b, gr):
                pe.wait_ge(s_exp, H * b + G * (gr + 1))
                if gr == 0:
                    pe.wait_ge(s_vaug, b + 1)
                    pe.wait_ge(s_max, H * (b + 1))
                for tt in range(NT):
                    for j in range(G):
                        h = G * gr + j
                        mm = pe.matmul(ps_s[gr // 2][32 * j:32 * j + 32, (gr % 2) * N:(gr % 2 + 1) * N],
                                       v_aug[b % 2][:, tt, h, :], probs[:, h % (2 * G), tt, :],
                                       start=(tt == 0), stop=(tt == NT - 1))
                mm.then_inc(s_pv, 1)

            def post(b):
                pe.wait_ge(s_oT, b + 1)
                pe.wait_ge(s_exp, H * (b + 1))
                for tt in range(NT):
                    for gr in range(G):
                        mm = pe.transpose(ps_t[tt][:, gr * P:(gr + 1) * P], oT[:, gr, tt * P:(tt + 1) * P], ident[:])
                mm.then_inc(s_oTp, 1)
                pe.wait_ge(s_on, b + 1)
                for c in range(NC):
                    for tt in range(NT):
                        mm = pe.transpose(ps_s[0][:, c * N + tt * P:c * N + (tt + 1) * P],
                                          o_n[:, tt, c * P:(c + 1) * P], ident[:])
                mm.then_inc(s_onTp, 1)
                pe.wait_ge(s_otlo, b + 1)
                for tt in range(NT):
                    t_ = slice(tt * P, (tt + 1) * P)
                    mm = product(half(ps_s[1], tt), [
                        pr for c in range(NC)
                        for pr in three(oT_hi[:, c, t_], oT_lo[:, c, t_], wa_hi[:, c, OP:OR], wa_lo[:, c, OP:OR])])
                mm.then_inc(s_proj, 1)
                pe.wait_ge(s_x2, b + 1)
                for c in range(NC):
                    for tt in range(NT):
                        mm = pe.transpose(ps_t[0][:, c * N + tt * P:c * N + (tt + 1) * P],
                                          x2[:, tt, c * P:(c + 1) * P], ident[:])
                mm.then_inc(s_x2Tp, 1)
                pe.wait_ge(s_x2hi, b + 1)
                pe.wait_ge(s_x2lo, b + 1)
                rt = slice(OR, OR + P)
                product(ps_t[1][:, 0:N], [
                    pr for c in range(NC)
                    for pr in three(wa_hi[:, c, rt], wa_lo[:, c, rt], x2T_hi[:, c, :], x2T_lo[:, c, :])
                ]).then_inc(s_lgTp, 1)
                pe.wait_ge(s_lgT, b + 1)
                for tt in range(NT):
                    mm = pe.transpose(ps_s[0][:, tt * E:(tt + 1) * E], lgT[:, tt * P:(tt + 1) * P], ident[0:E, 0:E])
                mm.then_inc(s_lgp, 1)
                pe.wait_ge(s_gate, b + 1)
                for tt in range(NT):
                    mm = pe.transpose(ps_t[1][0:E, tt * P:(tt + 1) * P], gate[:, tt, :], ident[:])
                mm.then_inc(s_gTp, 1)
                pe.wait_ge(s_gateT, b + 1)
                for tt in range(NT):
                    mm = pe.matmul(half(ps_s[1], tt), gateT[:, tt * P:(tt + 1) * P], bo[:], start=True, stop=True)
                mm.then_inc(s_bo, 1)

            def layer1(b, e):
                k = E * b + e
                if k == 0:
                    pe.wait_ge(s_wilo, 1)
                if e == 0 and b + 1 < B:
                    pe.wait_ge(s_vaug, b + 2)
                    pe.wait_ge(s_znT, b + 2)
                if k >= 2:
                    pe.wait_ge(s_gelu, k - 1)
                for hc in range(NC):
                    hs = slice(hc * P, (hc + 1) * P)
                    mm = product(half(ps_l1[e % 2], hc), [
                        pr for c in range(NC)
                        for pr in three(wi_hi[:, e, c, hs], wi_lo[:, e, c, hs], x2T_hi[:, c, :], x2T_lo[:, c, :])])
                mm.then_inc(s_l1, 1)

            def layer2(b, e):
                k = E * b + e
                pe.wait_ge(s_gelu, k + 1)
                if k == 0:
                    pe.wait_ge(d_wo, 16)
                if e == 0 and b + 1 < B:
                    pe.wait_ge(s_qkf, b + 2)
                if k >= 1:
                    pe.wait_ge(s_acc, NT * k)
                for tt in range(NT):
                    mm = product(half(ps_l2, tt), [(g[e % 2][:, hc, tt * P:(tt + 1) * P], wo[:, e, hc, :])
                                                   for hc in range(NC)])
                mm.then_inc(s_l2, 1)

            tok(0)
            zn_transposes(0)
            qkv(0)
            for t in range(B + 1):
                for e in range(E):
                    if t < B:
                        scores(t, 2 * e)
                        scores(t, 2 * e + 1)
                        if e == 4:
                            max_transposes(t, 0)
                    if t >= 1:
                        layer1(t - 1, e)
                        if e >= 1:
                            layer2(t - 1, e - 1)
                if t < B:
                    max_transposes(t, 1)
                if t >= 1:
                    layer2(t - 1, E - 1)
                if t == B:
                    break
                if t + 1 < B:
                    tok(t + 1)
                for h in range(H):
                    scores_t(t, h)
                    if h % G == G - 1 and h >= 2 * G - 1:
                        pv(t, h // G - 1)
                    if h == 7 and t + 1 < B:
                        zn_transposes(t + 1)
                    if h == 11 and t + 1 < B:
                        qkv(t + 1)
                pv(t, G - 1)
                post(t)


def ln_index(b, i):
    if i < 3:
        return i if b == 0 else 3 + 4 * (b - 1) + i
    return 3 + 4 * b + (3 if b + 1 < B else 0)


def kernel(x, L0_tok_W, L0_tok_gamma, L0_attn_ln_w, L0_attn_ln_b, L0_attn_W_qkv, L0_attn_b_qkv,
           L0_attn_W_proj, L0_attn_b_proj, L0_ffn_router_w, L0_ffn_w_in, L0_ffn_b_in, L0_ffn_w_out,
           L0_ffn_b_out):
    import numpy as np
    import concourse.bacc as bacc
    from concourse.bass_utils import run_bass_kernel_spmd

    f = lambda a: np.asarray(a)
    patches = f(x).reshape(B, 5, 16, 8, 16, 8).transpose(1, 3, 5, 0, 2, 4).reshape(320, B * N)

    def chunks(a):
        padded = np.zeros((KF * NF, a.shape[1]), a.dtype)
        padded[:320] = a
        return padded.reshape(NF, KF, -1).transpose(1, 0, 2)

    def rows(a):
        return a.reshape(NC, P, -1).transpose(1, 0, 2)

    wqkv, bqkv = f(L0_attn_W_qkv), f(L0_attn_b_qkv)
    order = lambda a: a.reshape(-1, 2, 8, 2, DH).transpose(0, 1, 3, 4, 2)
    arrays = {
        "xT": chunks(patches),
        "w_tok": chunks(f(L0_tok_W)),
        "gamma": f(L0_tok_gamma),
        "ln_w": f(L0_attn_ln_w).reshape(NC, P).T,
        "ln_b": f(L0_attn_ln_b).reshape(NC, P).T,
        "w_qk": rows(order(wqkv[:, :2 * D]).reshape(D, 4 * P)),
        "w_v": rows(wqkv[:, 2 * D:]),
        "b_qk": order(bqkv[None, :2 * D]).reshape(4, P).T,
        "b_v": bqkv[2 * D:],
        "w_proj": rows(f(L0_attn_W_proj)),
        "b_proj": f(L0_attn_b_proj),
        "w_router": rows(f(L0_ffn_router_w)),
        "w_in": f(L0_ffn_w_in).reshape(E, NC, P, D).transpose(2, 0, 1, 3),
        "b_in": f(L0_ffn_b_in).reshape(E, NC, P).transpose(2, 0, 1),
        "w_out": f(L0_ffn_w_out).reshape(E, NC, P, D).transpose(2, 0, 1, 3),
        "b_out": f(L0_ffn_b_out),
        "ident_c": np.eye(P, dtype=np.float32),
        "iota_c": np.tile(np.arange(E, dtype=np.float32), (P, 1)),
    }
    nc = bacc.Bacc("TRN2", target_bir_lowering=False, num_devices=1)
    ins, args = {}, []
    for name, a in arrays.items():
        ins[name + "_dram"] = np.ascontiguousarray(a)
        args.append(nc.dram_tensor(name + "_dram", a.shape, mybir.dt.from_np(a.dtype), kind="ExternalInput").ap())
    args.append(nc.dram_tensor("out_dram", (B, N, D), F32, kind="ExternalOutput").ap())
    build(nc, *args)
    r = run_bass_kernel_spmd(nc, [ins], core_ids=[0])
    return r.results[0]["out_dram"]
```

```python
from contextlib import ExitStack

import concourse.bass as bass
from concourse import mybir

F32 = mybir.dt.float32
F32R = mybir.dt.float32r
BF16 = mybir.dt.bfloat16
U32 = mybir.dt.uint32
ALU = mybir.AluOpType
ACT = mybir.ActivationFunctionType
AX = mybir.AxisListType.X

P = 128
B, N, D, H, DH, E = 4, 256, 256, 16, 16, 8
NT = N // P
NC = D // P
KF = 107
NF = 3
EPS = 1e-5
SCALE = DH ** -0.5
Q_PIECE = [0, 0, 1, 1, 0, 2]
K_PIECE = [0, 1, 0, 1, 2, 0]
SLOTS = len(Q_PIECE)
MROW = SLOTS * DH
KSC = MROW + 3
G = 4


def build(nc, xT, w_tok, w_attn, w_in, w_out, columns, row_params, b_out, out):
    with ExitStack() as ctx:
        def sb(name, shape, dt=F32):
            return ctx.enter_context(nc.sbuf_tensor(name, shape, dt))

        def sem(name):
            return ctx.enter_context(nc.semaphore(name))

        bank = [ctx.enter_context(nc.psum_tensor(f"bank{i}", [P, 512], F32)) for i in range(8)]
        ps_s, ps_t, ps_l1 = bank[0:2], bank[2:4], bank[4:6]
        ps_l2, ps_x = bank[6], bank[7]

        cols = sb("cols", [P, P + E + 2 * NC + 4 + E * NC])
        at = [0]

        def columns_of(n):
            at[0] += n
            return cols[:, at[0] - n:at[0]]

        ident, iota, lnw, lnb, bqk = (columns_of(n) for n in (P, E, NC, NC, 4))
        bin_ = columns_of(E * NC).rearrange("p (e c) -> p e c", c=NC)
        rowp = sb("rowp", [P, 3 * D])
        gam, bv, bp = (rowp[:, i * D:(i + 1) * D] for i in range(3))
        bo = sb("bo", [E, D])
        nhalf = sb("nhalf", [P, NT])
        wt_raw, wt_hi, wt_lo = sb("wt_raw", [KF, NF, D]), sb("wt_hi", [KF, NF, D], F32R), sb("wt_lo", [KF, NF, D], F32R)
        stage_a = sb("stage_a", [P, NC * (4 * P + 2 * D + E)])
        wa_raw = stage_a[:].rearrange("p (c n) -> p c n", c=NC)
        qk = stage_a[:, 0:4 * N].rearrange("p (m n) -> p m n", m=4)
        qk_r = stage_a[:, 4 * N:8 * N].rearrange("p (m n) -> p m n", m=4)
        wa_hi = sb("wa_hi", [P, NC, 4 * P + D + D + P], F32R)
        wa_lo = sb("wa_lo", [P, NC, 4 * P + D + D + P], F32R)
        OV, OP, OR = 4 * P, 4 * P + D, 4 * P + 2 * D
        stage_i = sb("stage_i", [P, E * NC * D])
        wi_raw = stage_i[:].rearrange("p (e c n) -> p e c n", e=E, c=NC)
        probs = stage_i[:].rearrange("p (h t n) -> p h t n", h=2 * G, t=NT)
        wi_hi = sb("wi_hi", [P, E, NC, D], F32R)
        wi_lo = sb("wi_lo", [P, E, NC, D], F32R)
        wo = sb("wo", [P, E, NC, D])

        x_raw = sb("x_raw", [KF, NF, N])
        x_hi = sb("x_hi", [KF, NF, N], F32R)
        x_lo = sb("x_lo", [KF, NF, N], F32R)
        stats = sb("stats", [P, NT, 6])
        mv = sb("mv", [P, NT, 2])
        var_eps = sb("var_eps", [P, NT])
        rstd = sb("rstd", [P, NT])
        h0 = sb("h0", [P, NT, D])
        z = sb("z", [P, NT, D])
        zn = sb("zn", [P, NT, D])
        x2 = zn
        resid = [sb(f"resid{i}", [P, NT, D]) for i in range(2)]
        znT = sb("znT", [P, NC, N])
        znT_hi, znT_lo = sb("znT_hi", [P, NC, N], F32R), sb("znT_lo", [P, NC, N], F32R)
        piece = [sb(f"piece{i}", [P, 4, N], BF16) for i in range(3)]
        q_st = [sb(f"q_st{i}", [P, H, N], BF16) for i in range(2)]
        k_st = [sb(f"k_st{i}", [P, H, N], BF16) for i in range(2)]
        v_aug = [sb(f"v_aug{i}", [P, NT, H, 2 * DH]) for i in range(2)]
        neg_max = sb("neg_max", [P, NT, H])
        m_row = sb("m_row", [H // 2, 3, N], BF16)
        m_rem = sb("m_rem", [H // 2, N])
        oT = sb("oT", [P, G, N])
        o_rs = sb("o_rs", [P, NT, H])
        o_n = oT[:, 0:NT, :]
        oT_hi, oT_lo = sb("oT_hi", [P, NC, N], F32R), sb("oT_lo", [P, NC, N], F32R)
        x2T_hi = [sb(f"x2T_hi{i}", [P, NC, N], F32R) for i in range(2)]
        x2T_lo = [sb(f"x2T_lo{i}", [P, NC, N], F32R) for i in range(2)]
        lgT = sb("lgT", [E, N])
        lg_max = sb("lg_max", [P, NT])
        ex = sb("ex", [P, NT, E])
        ex_sum = sb("ex_sum", [P, NT])
        ex_rs = sb("ex_rs", [P, NT])
        pr = sb("pr", [P, NT, E])
        top_p = sb("top_p", [P, NT, 8])
        top_i = sb("top_i", [P, NT, 8], U32)
        top_f = sb("top_f", [P, NT, 8])
        gate_a, gate_b = sb("gate_a", [P, NT, E]), sb("gate_b", [P, NT, E])
        gate = [sb(f"gate{i}", [P, NT, E]) for i in range(2)]
        gateT = sb("gateT", [E, N])
        acc = [sb(f"acc{i}", [P, NT, D]) for i in range(2)]
        g = [sb(f"g{i}", [P, NC, N]) for i in range(2)]

        d_x = sem("d_x")
        d_wt, d_wa, d_wi, d_wo, d_out = sem("d_wt"), sem("d_wa"), sem("d_wi"), sem("d_wo"), sem("d_out")
        d_cols, d_rowp, d_bo = sem("d_cols"), sem("d_rowp"), sem("d_bo")
        d_stack = [sem(f"d_stack{i}") for i in range(2)]
        d_m = [sem(f"d_m{i}") for i in range(2)]
        dve_own, s_xlo, s_wt, s_wa, s_wihi = sem("dve_own"), sem("s_xlo"), sem("s_wt"), sem("s_wa"), sem("s_wihi")
        s_mv, s_zn, s_vaug, s_max, s_mrow = sem("s_mv"), sem("s_zn"), sem("s_vaug"), sem("s_max"), sem("s_mrow")
        s_resid, s_on, s_otlo, s_x2, s_x2lo = sem("s_resid"), sem("s_on"), sem("s_otlo"), sem("s_x2"), sem("s_x2lo")
        s_lgmax, s_gate, s_gateT, s_accini, s_acc = sem("s_lgmax"), sem("s_gate"), sem("s_gateT"), sem("s_accini"), sem("s_acc")
        s_ones, s_p1, s_wahi = sem("s_ones"), sem("s_p1"), sem("s_wahi")
        s_tok, s_znTp, s_qkp, s_vp = sem("s_tok"), sem("s_znTp"), sem("s_qkp"), sem("s_vp")
        s_S, s_mT, s_ST, s_pv = sem("s_S"), sem("s_mT"), sem("s_ST"), sem("s_pv")
        s_oTp, s_onTp, s_proj, s_x2Tp = sem("s_oTp"), sem("s_onTp"), sem("s_proj"), sem("s_x2Tp")
        s_lgTp, s_lgp, s_gTp, s_bo = sem("s_lgTp"), sem("s_lgp"), sem("s_gTp"), sem("s_bo")
        s_l1, s_l2 = sem("s_l1"), sem("s_l2")
        s_znT, s_p0, s_qkf, s_exp = sem("s_znT"), sem("s_p0"), sem("s_qkf"), sem("s_exp")
        s_oT, s_othi, s_x2hi, s_lgT, s_ex, s_gelu = sem("s_oT"), sem("s_othi"), sem("s_x2hi"), sem("s_lgT"), sem("s_ex"), sem("s_gelu")
        pool_own, s_rstd, s_znhi, s_znlo, s_wilo, s_nhalf = (
            sem("pool_own"), sem("s_rstd"), sem("s_znhi"), sem("s_znlo"), sem("s_wilo"), sem("s_nhalf"))
        s_rem, s_p2 = sem("s_rem"), sem("s_p2")

        STACKED = 16 * 2 * SLOTS
        out_v = out.rearrange("b (t p) d -> b p t d", p=P)

        def half(bk, i):
            return bk[:, i * N:(i + 1) * N]

        def both(bk):
            return bk[:, :].rearrange("p (t n) -> p t n", n=N)

        def two(i):
            return slice(2 * i, 2 * i + 2)

        block = ctx.enter_context(nc.Block())

        @block.sync
        def _(sp):
            def load_x(b):
                if b >= 1:
                    sp.wait_ge(s_xlo, b)
                sp.dma_start(x_raw[:], xT[:, :, b * N:(b + 1) * N]).then_inc(d_x, 16)

            def stack(b):
                if b >= 2:
                    sp.wait_ge(s_ST, H * (b - 1))
                for i, (st, table) in enumerate(((q_st[b % 2], Q_PIECE), (k_st[b % 2], K_PIECE))):
                    for pc, made in enumerate((s_p0, s_p1, s_p2)):
                        sp.wait_ge(made, 2 * b + i + 1)
                        for s in range(SLOTS):
                            if table[s] == pc:
                                dst = st[s * DH:(s + 1) * DH, :, :].rearrange("d (h m) n -> d h (m n)", m=2)
                                sp.dma_start(dst, piece[pc][:, two(i), :]).then_inc(d_stack[b % 2], 16)

            def max_rows(b, hh):
                sp.wait_ge(s_mrow, 2 * b + hh + 1)
                for r in range(3):
                    sp.dma_start(q_st[b % 2][MROW + r:MROW + r + 1, hh * 8:hh * 8 + 8, :],
                                 m_row[:, r, :]).then_inc(d_m[hh], 16)

            sp.dma_start(wt_raw[:], w_tok).then_inc(d_wt, 16)
            load_x(0)
            sp.dma_start(stage_a[:], w_attn).then_inc(d_wa, 16)
            sp.dma_start(stage_i[:], w_in).then_inc(d_wi, 16)
            load_x(1)
            sp.dma_start(wo[:], w_out).then_inc(d_wo, 16)
            stack(0)
            for t in range(B + 1):
                if t < B:
                    for hh in range(2):
                        max_rows(t, hh)
                if t + 2 < B:
                    load_x(t + 2)
                if t + 1 < B:
                    stack(t + 1)
                if t >= 1:
                    sp.wait_ge(s_acc, NT * E * t)
                    sp.dma_start(out_v[t - 1], acc[(t - 1) % 2][:]).then_inc(d_out, 16)
            sp.wait_ge(d_out, 16 * B)

        @block.gpsimd
        def _(pool):
            n_own = [0]

            def link(ins):
                n_own[0] += 1
                ins.then_inc(pool_own, 1)
                pool.wait_ge(pool_own, n_own[0])

            def rsqrt(k):
                pool.wait_ge(s_mv, k + 1)
                link(pool.tensor_scalar(var_eps[:], mv[:, :, 1], EPS, None, ALU.add))
                pool.tensor_tensor(rstd[:], var_eps[:], nhalf[:], ALU.pow).then_inc(s_rstd, 1)

            def zn_low(b):
                pool.wait_ge(s_znhi, b + 1)
                pool.wait_ge(s_znT, b + 1)
                if b >= 1:
                    pool.wait_ge(s_vp, b)
                pool.tensor_tensor(znT_lo[:], znT[:], znT_hi[:].bitcast(F32), ALU.subtract).then_inc(s_znlo, 1)

            def remainders(b, i):
                pool.wait_ge(s_p0, 2 * b + i + 1)
                pool.wait_ge(s_qkf, 2 * b + i + 1)
                if b >= 1:
                    pool.wait_ge(s_p2, 2 * (b - 1) + i + 1)
                pool.tensor_tensor(qk_r[:, two(i), :], qk[:, two(i), :], piece[0][:, two(i), :],
                                   ALU.subtract).then_inc(s_rem, 1)
                pool.wait_ge(s_p1, 2 * b + i + 1)
                pool.tensor_tensor(piece[2][:, two(i), :], qk_r[:, two(i), :], piece[1][:, two(i), :],
                                   ALU.subtract).then_inc(s_p2, 1)

            pool.memset(nhalf[:], -0.5).then_inc(s_nhalf, 1)
            pool.wait_ge(s_nhalf, 1)
            for i in range(2):
                pool.memset(v_aug[i][:, :, :, DH:2 * DH], 1.0).then_inc(s_ones, 1)
                pool.wait_ge(s_ones, 2 * i + 1)
                pool.memset(k_st[i][MROW:KSC, :, :], 1.0).then_inc(s_ones, 1)
                pool.wait_ge(s_ones, 2 * i + 2)
            for i in range(3):
                rsqrt(ln_index(0, i))
            zn_low(0)
            remainders(0, 0)
            remainders(0, 1)
            pool.wait_ge(s_wihi, 1)
            pool.tensor_tensor(wi_lo[:], wi_raw, wi_hi[:].bitcast(F32), ALU.subtract).then_inc(s_wilo, 1)
            for t in range(B):
                if t + 1 < B:
                    for i in range(3):
                        rsqrt(ln_index(t + 1, i))
                    zn_low(t + 1)
                    remainders(t + 1, 0)
                rsqrt(ln_index(t, 3))
                if t + 1 < B:
                    remainders(t + 1, 1)

        @block.scalar
        def _(act):
            act.dma_start(cols[:], columns).then_inc(d_cols, 16)
            act.dma_start(rowp[:], row_params.partition_broadcast(P)).then_inc(d_rowp, 16)
            act.dma_start(bo[:], b_out).then_inc(d_bo, 16)

            def znT_out(b):
                act.wait_ge(s_znTp, b + 1)
                if b == 0:
                    act.wait_ge(d_cols, 16)
                if b >= 1:
                    act.wait_ge(s_znlo, b)
                act.activation(znT[:, 0, :], half(ps_x, 0), ACT.Identity, bias=lnb[:, 0:1], scale=lnw[:, 0:1])
                act.activation(znT[:, 1, :], half(ps_x, 1), ACT.Identity, bias=lnb[:, 1:2],
                               scale=lnw[:, 1:2]).then_inc(s_znT, 1)

            def qk_out(b, i):
                act.wait_ge(s_qkp, 2 * b + i + 1)
                if b >= 1:
                    act.wait_ge(d_stack[(b - 1) % 2], STACKED * ((b - 1) // 2 + 1))
                    act.wait_ge(s_rem, 2 * (b - 1) + i + 1)
                for m in range(2):
                    last = act.activation(piece[0][:, 2 * i + m, :], half(ps_x, m), ACT.Identity,
                                          bias=bqk[:, 2 * i + m:2 * i + m + 1])
                last.then_inc(s_p0, 1)
                for m in range(2):
                    last = act.activation(qk[:, 2 * i + m, :], half(ps_x, m), ACT.Identity,
                                          bias=bqk[:, 2 * i + m:2 * i + m + 1])
                last.then_inc(s_qkf, 1)

            def exp(b, h):
                act.wait_ge(s_ST, H * b + h + 1)
                if b == 0 and h == 0:
                    act.wait_ge(s_wilo, 1)
                if H * b + h >= 2 * G:
                    act.wait_ge(s_pv, (H * b + h - 2 * G) // G + 1)
                act.activation(probs[:, h % (2 * G), :, :], both(ps_t[h % 2]), ACT.Exp, scale=SCALE).then_inc(s_exp, 1)

            def o_out(b):
                act.wait_ge(s_pv, G * (b + 1))
                if b >= 1:
                    act.wait_ge(s_onTp, b)
                for i in range(2):
                    last = act.activation(oT[:, 2 * i:2 * i + 2, :], both(ps_s[i]), ACT.Copy)
                last.then_inc(s_oT, 1)

            def oT_high(b):
                act.wait_ge(s_onTp, b + 1)
                if b >= 1:
                    act.wait_ge(s_proj, b)
                act.activation(oT_hi[:], both(ps_s[0]), ACT.Copy).then_inc(s_othi, 1)

            def x2T_high(b):
                act.wait_ge(s_x2Tp, b + 1)
                if b >= 2:
                    act.wait_ge(s_l1, E * (b - 1))
                act.activation(x2T_hi[b % 2][:], both(ps_t[0]), ACT.Copy).then_inc(s_x2hi, 1)

            def logits(b):
                act.wait_ge(s_lgTp, b + 1)
                if b >= 1:
                    act.wait_ge(s_lgp, b)
                act.activation(lgT[:], ps_t[1][0:E, 0:N], ACT.Copy).then_inc(s_lgT, 1)

            def logits_exp(b):
                act.wait_ge(s_lgmax, b + 1)
                for tt in range(NT):
                    last = act.activation(ex[:, tt, :], ps_t[0][:, tt * E:(tt + 1) * E], ACT.Exp, bias=lg_max[:, tt:tt + 1])
                last.then_inc(s_ex, 1)

            def gelu(b, e):
                k = E * b + e
                act.wait_ge(s_l1, k + 1)
                if k >= 2:
                    act.wait_ge(s_l2, k - 1)
                for hc in range(NC):
                    last = act.activation(g[e % 2][:, hc, :], half(ps_l1[e % 2], hc), ACT.Gelu_apprx_tanh,
                                          bias=bin_[:, e, hc:hc + 1])
                last.then_inc(s_gelu, 1)

            act.wait_ge(d_wa, 16)
            act.activation(wa_hi[:, :, 0:OR + E], wa_raw, ACT.Copy).then_inc(s_wahi, 1)
            znT_out(0)
            qk_out(0, 0)
            qk_out(0, 1)
            act.wait_ge(d_wi, 16)
            act.activation(wi_hi[:], wi_raw, ACT.Copy).then_inc(s_wihi, 1)
            for t in range(B + 1):
                now, front, moe = t < B, t + 1 < B, t >= 1
                if moe:
                    for e in range(4):
                        gelu(t - 1, e)
                if now:
                    for h in range(H):
                        exp(t, h)
                if now:
                    o_out(t)
                if front:
                    znT_out(t + 1)
                if moe:
                    gelu(t - 1, 4)
                if now:
                    oT_high(t)
                if front:
                    qk_out(t + 1, 0)
                if moe:
                    gelu(t - 1, 5)
                if front:
                    qk_out(t + 1, 1)
                if moe:
                    gelu(t - 1, 6)
                if now:
                    x2T_high(t)
                    logits(t)
                if moe:
                    gelu(t - 1, 7)
                if now:
                    logits_exp(t)

        @block.vector
        def _(dve):
            n_own = [0]

            def link(ins):
                n_own[0] += 1
                ins.then_inc(dve_own, 1)
                dve.wait_ge(dve_own, n_own[0])

            def moments(src, k):
                for tt in range(NT):
                    ins = dve.bn_stats(stats[:, tt, :], src[:, tt, :])
                link(ins)
                if k >= 1:
                    dve.wait_ge(s_rstd, k)
                for tt in range(NT):
                    ins = dve.bn_aggr(mv[:, tt, :], stats[:, tt, :])
                ins.then_inc(s_mv, 1)
                dve.wait_ge(s_rstd, k + 1)

            def normed(dst, src):
                for tt in range(NT):
                    ins = dve.tensor_scalar(dst[:, tt, :], src[:, tt, :], mv[:, tt, 0:1], rstd[:, tt:tt + 1],
                                            ALU.subtract, ALU.mult)
                return ins

            def split_x(b):
                dve.wait_ge(d_x, 16 * (b + 1))
                if b >= 1:
                    dve.wait_ge(s_tok, b)
                link(dve.tensor_copy(x_hi[:], x_raw[:]))
                dve.tensor_tensor(x_lo[:], x_raw[:], x_hi[:].bitcast(F32), ALU.subtract).then_inc(s_xlo, 1)

            def norms(b):
                dve.wait_ge(s_tok, b + 1)
                tok = both(ps_x)
                moments(tok, ln_index(b, 0))
                link(normed(z, tok))
                if b == 0:
                    dve.wait_ge(d_rowp, 16)
                for tt in range(NT):
                    ins = dve.tensor_tensor(h0[:, tt, :], z[:, tt, :], gam, ALU.mult)
                link(ins)
                moments(h0, ln_index(b, 1))
                link(normed(z, h0))
                moments(z, ln_index(b, 2))
                if b >= 1:
                    dve.wait_ge(s_znTp, b)
                if b >= 2:
                    dve.wait_ge(s_x2Tp, b - 1)
                normed(zn, z).then_inc(s_zn, 1)
                dve.wait_ge(s_zn, b + 1)
                link(dve.tensor_tensor(z[:], z[:], h0[:], ALU.add))
                for tt in range(NT):
                    ins = dve.tensor_tensor(resid[b % 2][:, tt, :], z[:, tt, :], bp, ALU.add)
                ins.then_inc(s_resid, 1)
                dve.wait_ge(s_resid, b + 1)

            def zn_high(b):
                dve.wait_ge(s_znT, b + 1)
                if b >= 1:
                    dve.wait_ge(s_vp, b)
                dve.tensor_copy(znT_hi[:], znT[:]).then_inc(s_znhi, 1)

            def second_piece(b, i):
                dve.wait_ge(s_rem, 2 * b + i + 1)
                if b >= 1:
                    dve.wait_ge(d_stack[(b - 1) % 2], STACKED * ((b - 1) // 2 + 1))
                dve.tensor_copy(piece[1][:, two(i), :], qk_r[:, two(i), :]).then_inc(s_p1, 1)

            def v_out(b):
                dve.wait_ge(s_vp, b + 1)
                if b == 0:
                    dve.wait_ge(s_ones, 4)
                    dve.wait_ge(d_rowp, 16)
                if b >= 2:
                    dve.wait_ge(s_pv, G * (b - 1))
                for tt in range(NT):
                    ins = dve.tensor_tensor(v_aug[b % 2][:, tt, :, 0:DH],
                                            half(ps_x, tt).rearrange("p (h d) -> p h d", d=DH),
                                            bv.rearrange("p (h d) -> p h d", d=DH), ALU.add)
                ins.then_inc(s_vaug, 1)

            def head_max(b, h):
                dve.wait_ge(s_S, H * b + h + 1)
                if h == 0 and b >= 1:
                    dve.wait_ge(s_mT, 2 * b)
                dve.tensor_reduce(neg_max[:, :, h], both(ps_s[h % 2]), AX, ALU.max, negate=True).then_inc(s_max, 1)

            def max_pieces(b, hh):
                k = 2 * b + hh
                dve.wait_ge(s_mT, k + 1)
                if k >= 1:
                    dve.wait_ge(d_m[(k - 1) % 2], 48 * ((k - 1) // 2 + 1))
                src = ps_x[0:H // 2, 0:N]
                link(dve.tensor_copy(m_row[:, 0, :], src))
                link(dve.tensor_tensor(m_rem[:], src, m_row[:, 0, :], ALU.subtract))
                link(dve.tensor_copy(m_row[:, 1, :], m_rem[:]))
                dve.tensor_tensor(m_row[:, 2, :], m_rem[:], m_row[:, 1, :], ALU.subtract).then_inc(s_mrow, 1)

            def add_expert(b, e):
                k = E * b + e
                dve.wait_ge(s_l2, k + 1)
                a = acc[b % 2]
                if e == 0:
                    dve.wait_ge(s_accini, b + 1)
                else:
                    dve.wait_ge(s_acc, NT * k)
                for tt in range(NT):
                    dve.scalar_tensor_tensor(out=a[:, tt, :], in0=half(ps_l2, tt), scalar=gate[b % 2][:, tt, e:e + 1],
                                             in1=a[:, tt, :], op0=ALU.mult, op1=ALU.add).then_inc(s_acc, 1)

            def normalise(b):
                dve.wait_ge(s_oTp, b + 1)
                heads = [ps_t[tt][:, :].rearrange("p (h d) -> p h d", d=2 * DH) for tt in range(NT)]
                for tt in range(NT):
                    ins = dve.reciprocal(o_rs[:, tt, :], heads[tt][:, :, DH])
                link(ins)
                for tt in range(NT):
                    ins = dve.tensor_tensor(o_n[:, tt, :].rearrange("p (h d) -> p h d", d=DH), heads[tt][:, :, 0:DH],
                                            o_rs[:, tt, :].unsqueeze(2).to_broadcast([P, H, DH]), ALU.mult)
                ins.then_inc(s_on, 1)

            def oT_low(b):
                dve.wait_ge(s_othi, b + 1)
                dve.tensor_tensor(oT_lo[:], both(ps_s[0]), oT_hi[:].bitcast(F32), ALU.subtract).then_inc(s_otlo, 1)

            def attn_out(b):
                h1 = acc[b % 2]
                dve.wait_ge(s_proj, b + 1)
                if b >= 2:
                    dve.wait_ge(d_out, 16 * (b - 1))
                link(dve.tensor_tensor(h1[:], both(ps_s[1]), resid[b % 2][:], ALU.add))
                moments(h1, ln_index(b, 3))
                dve.wait_ge(s_znTp, min(b + 2, B))
                if b >= 1:
                    dve.wait_ge(s_x2Tp, b)
                normed(x2, h1).then_inc(s_x2, 1)

            def x2T_low(b):
                dve.wait_ge(s_x2hi, b + 1)
                dve.tensor_tensor(x2T_lo[b % 2][:], both(ps_t[0]), x2T_hi[b % 2][:].bitcast(F32),
                                  ALU.subtract).then_inc(s_x2lo, 1)

            def logits_max(b):
                dve.wait_ge(s_lgp, b + 1)
                lg = ps_t[0][:, 0:NT * E].rearrange("p (t e) -> p t e", e=E)
                dve.tensor_reduce(lg_max[:], lg, AX, ALU.max, negate=True).then_inc(s_lgmax, 1)

            def gates(b):
                dve.wait_ge(s_ex, b + 1)
                link(dve.tensor_reduce(ex_sum[:], ex[:], AX, ALU.add))
                link(dve.reciprocal(ex_rs[:], ex_sum[:]))
                link(dve.tensor_tensor(pr[:], ex[:], ex_rs[:].unsqueeze(2).to_broadcast([P, NT, E]), ALU.mult))
                for tt in range(NT):
                    ins = dve.max(top_p[:, tt, :], pr[:, tt, :])
                link(ins)
                for tt in range(NT):
                    ins = dve.max_index(top_i[:, tt, :], top_p[:, tt, :], pr[:, tt, :])
                link(ins)
                link(dve.tensor_copy(top_f[:], top_i[:]))
                if b == 0:
                    dve.wait_ge(d_cols, 16)
                for tt in range(NT):
                    for i, dst in enumerate((gate_a, gate_b)):
                        ins = dve.tensor_scalar(dst[:, tt, :], iota, top_f[:, tt, i:i + 1], top_p[:, tt, i:i + 1],
                                                ALU.is_equal, ALU.mult)
                link(ins)
                dve.tensor_tensor(gate[b % 2][:], gate_a[:], gate_b[:], ALU.add).then_inc(s_gate, 1)

            def gates_transposed(b):
                dve.wait_ge(s_gTp, b + 1)
                dve.tensor_copy(gateT[:], ps_t[1][0:E, 0:N]).then_inc(s_gateT, 1)

            def first_acc(b):
                dve.wait_ge(s_bo, b + 1)
                dve.tensor_tensor(acc[b % 2][:], both(ps_t[0]), acc[b % 2][:], ALU.add).then_inc(s_accini, 1)

            dve.wait_ge(d_wt, 16)
            link(dve.tensor_copy(wt_hi[:], wt_raw[:]))
            dve.tensor_tensor(wt_lo[:], wt_raw[:], wt_hi[:].bitcast(F32), ALU.subtract).then_inc(s_wt, 1)
            split_x(0)
            link(dve.memset(wa_hi[:, :, OR + E:OR + P].bitcast(F32), 0.0))
            link(dve.memset(wa_lo[:, :, OR + E:OR + P].bitcast(F32), 0.0))
            norms(0)
            zn_high(0)
            dve.wait_ge(s_wahi, 1)
            dve.tensor_tensor(wa_lo[:, :, 0:OR + E], wa_raw, wa_hi[:, :, 0:OR + E].bitcast(F32),
                              ALU.subtract).then_inc(s_wa, 1)
            second_piece(0, 0)
            second_piece(0, 1)
            v_out(0)
            for t in range(B + 1):
                now, front, moe = t < B, t + 1 < B, t >= 1
                def heads(h, t=t):
                    if t < B:
                        head_max(t, h)
                        head_max(t, h + 1)

                heads(0)
                if moe:
                    gates(t - 1)
                heads(2)
                if moe:
                    gates_transposed(t - 1)
                heads(4)
                if moe:
                    first_acc(t - 1)
                heads(6)
                if moe:
                    add_expert(t - 1, 0)
                heads(8)
                if now:
                    max_pieces(t, 0)
                heads(10)
                if moe:
                    add_expert(t - 1, 1)
                heads(12)
                if front:
                    split_x(t + 1)
                heads(14)
                if moe:
                    add_expert(t - 1, 2)
                if now:
                    max_pieces(t, 1)
                if moe:
                    add_expert(t - 1, 3)
                if front:
                    norms(t + 1)
                if now:
                    normalise(t)
                if front:
                    zn_high(t + 1)
                if now:
                    oT_low(t)
                if front:
                    second_piece(t + 1, 0)
                if now:
                    attn_out(t)
                if front:
                    second_piece(t + 1, 1)
                if moe:
                    add_expert(t - 1, 4)
                if now:
                    x2T_low(t)
                if front:
                    v_out(t + 1)
                if moe:
                    add_expert(t - 1, 5)
                if now:
                    logits_max(t)
                if moe:
                    add_expert(t - 1, 6)
                    add_expert(t - 1, 7)

        @block.tensor
        def _(pe):
            def product(o, pairs):
                for i, (w, x) in enumerate(pairs):
                    mm = pe.matmul(o, w, x, start=(i == 0), stop=(i == len(pairs) - 1))
                return mm

            def three(w_hi, w_lo, x_hi_, x_lo_):
                return [(w_hi, x_hi_), (w_lo, x_hi_), (w_hi, x_lo_)]

            def tok(b):
                pe.wait_ge(s_xlo, b + 1)
                if b == 0:
                    pe.wait_ge(s_wt, 1)
                if b >= 1:
                    pe.wait_ge(s_mrow, 2 * b)
                for tt in range(NT):
                    c = slice(tt * P, (tt + 1) * P)
                    mm = product(half(ps_x, tt), [
                        pr for f in range(NF)
                        for pr in three(x_hi[:, f, c], x_lo[:, f, c], wt_hi[:, f, :], wt_lo[:, f, :])])
                mm.then_inc(s_tok, 1)

            def zn_transposes(b):
                pe.wait_ge(s_zn, b + 1)
                if b == 0:
                    pe.wait_ge(d_cols, 16)
                for c in range(NC):
                    for tt in range(NT):
                        mm = pe.transpose(ps_x[:, c * N + tt * P:c * N + (tt + 1) * P],
                                          zn[:, tt, c * P:(c + 1) * P], ident)
                mm.then_inc(s_znTp, 1)

            def qk_product(b, i):
                if i == 0:
                    pe.wait_ge(s_znhi, b + 1)
                    pe.wait_ge(s_znlo, b + 1)
                    if b == 0:
                        pe.wait_ge(s_wa, 1)
                else:
                    pe.wait_ge(s_p0, 2 * b + 1)
                    pe.wait_ge(s_qkf, 2 * b + 1)
                for m in range(2):
                    cs = slice((2 * i + m) * P, (2 * i + m + 1) * P)
                    mm = product(half(ps_x, m), [
                        pr for c in range(NC)
                        for pr in three(wa_hi[:, c, cs], wa_lo[:, c, cs], znT_hi[:, c, :], znT_lo[:, c, :])])
                mm.then_inc(s_qkp, 1)

            def v_product(b):
                pe.wait_ge(s_p0, 2 * b + 2)
                pe.wait_ge(s_qkf, 2 * b + 2)
                for tt in range(NT):
                    t_ = slice(tt * P, (tt + 1) * P)
                    mm = product(half(ps_x, tt), [
                        pr for c in range(NC)
                        for pr in three(znT_hi[:, c, t_], znT_lo[:, c, t_], wa_hi[:, c, OV:OP], wa_lo[:, c, OV:OP])])
                mm.then_inc(s_vp, 1)

            def scores(b, h):
                if h == 0:
                    pe.wait_ge(d_stack[b % 2], STACKED * (b // 2 + 1))
                    if b >= 1:
                        pe.wait_ge(s_x2, b)
                if H * b + h >= 2:
                    pe.wait_ge(s_max, H * b + h - 1)
                for tt in range(NT):
                    mm = pe.matmul(half(ps_s[h % 2], tt), q_st[b % 2][0:MROW, h, tt * P:(tt + 1) * P],
                                   k_st[b % 2][0:MROW, h, :], start=True, stop=True)
                mm.then_inc(s_S, 1)

            def max_transposes(b, hh):
                pe.wait_ge(s_max, H * b + 8 * hh + 8)
                if hh == 0:
                    pe.wait_ge(s_vaug, b + 1)
                else:
                    pe.wait_ge(s_mrow, 2 * b + 1)
                for tt in range(NT):
                    mm = pe.transpose(ps_x[0:H // 2, tt * P:(tt + 1) * P], neg_max[:, tt, 8 * hh:8 * hh + 8], ident)
                mm.then_inc(s_mT, 1)

            def scores_t(b, h):
                if h % 8 == 0:
                    pe.wait_ge(d_m[h // 8], 48 * (b + 1))
                if h == 0 and b == 0:
                    pe.wait_ge(s_ones, 4)
                if h == 0 and b >= 1:
                    pe.wait_ge(s_accini, b)
                if H * b + h >= 2:
                    pe.wait_ge(s_exp, H * b + h - 1)
                for tt in range(NT):
                    mm = pe.matmul(half(ps_t[h % 2], tt), k_st[b % 2][0:KSC, h, tt * P:(tt + 1) * P],
                                   q_st[b % 2][0:KSC, h, :], start=True, stop=True)
                mm.then_inc(s_ST, 1)

            def pv(b, gr):
                pe.wait_ge(s_exp, H * b + G * (gr + 1))
                if gr == 0:
                    pe.wait_ge(s_vaug, b + 1)
                    pe.wait_ge(s_max, H * (b + 1))
                for tt in range(NT):
                    for j in range(G):
                        h = G * gr + j
                        mm = pe.matmul(ps_s[gr // 2][32 * j:32 * j + 32, (gr % 2) * N:(gr % 2 + 1) * N],
                                       v_aug[b % 2][:, tt, h, :], probs[:, h % (2 * G), tt, :],
                                       start=(tt == 0), stop=(tt == NT - 1))
                mm.then_inc(s_pv, 1)

            def o_transposes(b):
                pe.wait_ge(s_oT, b + 1)
                pe.wait_ge(s_exp, H * (b + 1))
                for tt in range(NT):
                    for gr in range(G):
                        mm = pe.transpose(ps_t[tt][:, gr * P:(gr + 1) * P], oT[:, gr, tt * P:(tt + 1) * P], ident)
                mm.then_inc(s_oTp, 1)

            def on_transposes(b):
                pe.wait_ge(s_on, b + 1)
                for c in range(NC):
                    for tt in range(NT):
                        mm = pe.transpose(ps_s[0][:, c * N + tt * P:c * N + (tt + 1) * P],
                                          o_n[:, tt, c * P:(c + 1) * P], ident)
                mm.then_inc(s_onTp, 1)

            def projection(b):
                pe.wait_ge(s_othi, b + 1)
                pe.wait_ge(s_otlo, b + 1)
                for tt in range(NT):
                    t_ = slice(tt * P, (tt + 1) * P)
                    mm = product(half(ps_s[1], tt), [
                        pr for c in range(NC)
                        for pr in three(oT_hi[:, c, t_], oT_lo[:, c, t_], wa_hi[:, c, OP:OR], wa_lo[:, c, OP:OR])])
                mm.then_inc(s_proj, 1)

            def x2_transposes(b):
                pe.wait_ge(s_x2, b + 1)
                for c in range(NC):
                    for tt in range(NT):
                        mm = pe.transpose(ps_t[0][:, c * N + tt * P:c * N + (tt + 1) * P],
                                          x2[:, tt, c * P:(c + 1) * P], ident)
                mm.then_inc(s_x2Tp, 1)

            def router(b):
                pe.wait_ge(s_x2hi, b + 1)
                pe.wait_ge(s_x2lo, b + 1)
                rt = slice(OR, OR + P)
                product(ps_t[1][:, 0:N], [
                    pr for c in range(NC)
                    for pr in three(wa_hi[:, c, rt], wa_lo[:, c, rt], x2T_hi[b % 2][:, c, :], x2T_lo[b % 2][:, c, :])
                ]).then_inc(s_lgTp, 1)

            def logits_transposes(b):
                pe.wait_ge(s_lgT, b + 1)
                for tt in range(NT):
                    mm = pe.transpose(ps_t[0][:, tt * E:(tt + 1) * E], lgT[:, tt * P:(tt + 1) * P], ident[0:E, 0:E])
                mm.then_inc(s_lgp, 1)

            def gate_transposes(b):
                pe.wait_ge(s_gate, b + 1)
                for tt in range(NT):
                    mm = pe.transpose(ps_t[1][0:E, tt * P:(tt + 1) * P], gate[b % 2][:, tt, :], ident)
                mm.then_inc(s_gTp, 1)

            def b_out_product(b):
                pe.wait_ge(s_gateT, b + 1)
                if b == 0:
                    pe.wait_ge(d_bo, 16)
                for tt in range(NT):
                    mm = pe.matmul(half(ps_t[0], tt), gateT[:, tt * P:(tt + 1) * P], bo[:], start=True, stop=True)
                mm.then_inc(s_bo, 1)

            def layer1(b, e):
                k = E * b + e
                if k == 0:
                    pe.wait_ge(s_wilo, 1)
                if k >= 2:
                    pe.wait_ge(s_gelu, k - 1)
                for hc in range(NC):
                    hs = slice(hc * P, (hc + 1) * P)
                    mm = product(half(ps_l1[e % 2], hc), [
                        pr for c in range(NC)
                        for pr in three(wi_hi[:, e, c, hs], wi_lo[:, e, c, hs],
                                        x2T_hi[b % 2][:, c, :], x2T_lo[b % 2][:, c, :])])
                mm.then_inc(s_l1, 1)

            def layer2(b, e):
                k = E * b + e
                pe.wait_ge(s_gelu, k + 1)
                if k == 0:
                    pe.wait_ge(d_wo, 16)
                if k >= 1:
                    pe.wait_ge(s_acc, NT * k)
                for tt in range(NT):
                    mm = product(half(ps_l2, tt), [(g[e % 2][:, hc, tt * P:(tt + 1) * P], wo[:, e, hc, :])
                                                   for hc in range(NC)])
                mm.then_inc(s_l2, 1)

            tok(0)
            zn_transposes(0)
            qk_product(0, 0)
            qk_product(0, 1)
            v_product(0)
            for t in range(B + 1):
                now, front, moe = t < B, t + 1 < B, t >= 1
                def heads(h, t=t):
                    if t < B:
                        scores(t, h)
                        scores(t, h + 1)

                heads(0)
                if moe:
                    layer1(t - 1, 0)
                heads(2)
                if moe:
                    layer1(t - 1, 1)
                    gate_transposes(t - 1)
                heads(4)
                if moe:
                    b_out_product(t - 1)
                    layer2(t - 1, 0)
                heads(6)
                if moe:
                    layer1(t - 1, 2)
                heads(8)
                if now:
                    max_transposes(t, 0)
                if moe:
                    layer2(t - 1, 1)
                heads(10)
                if moe:
                    layer1(t - 1, 3)
                heads(12)
                if moe:
                    layer2(t - 1, 2)
                heads(14)
                if moe:
                    layer2(t - 1, 3)
                if now:
                    max_transposes(t, 1)
                if front:
                    tok(t + 1)
                if moe and not now:
                    layer1(t - 1, 4)
                    layer1(t - 1, 5)
                if now:
                    for h in range(H):
                        scores_t(t, h)
                        if h % G == G - 1 and h >= 2 * G - 1:
                            pv(t, h // G - 1)
                        if moe and h in (3, 9):
                            layer1(t - 1, 4 + h // 6)
                    pv(t, G - 1)
                if now:
                    o_transposes(t)
                if front:
                    zn_transposes(t + 1)
                if now:
                    on_transposes(t)
                if front:
                    qk_product(t + 1, 0)
                if now:
                    projection(t)
                if front:
                    qk_product(t + 1, 1)
                if moe:
                    layer2(t - 1, 4)
                    layer1(t - 1, 6)
                if now:
                    x2_transposes(t)
                if front:
                    v_product(t + 1)
                if now:
                    router(t)
                if moe:
                    layer2(t - 1, 5)
                    layer1(t - 1, 7)
                if now:
                    logits_transposes(t)
                if moe:
                    layer2(t - 1, 6)
                    layer2(t - 1, 7)


def ln_index(b, i):
    if i < 3:
        return i if b == 0 else 3 + 4 * (b - 1) + i
    return 3 + 4 * b + (3 if b + 1 < B else 0)


def kernel(x, L0_tok_W, L0_tok_gamma, L0_attn_ln_w, L0_attn_ln_b, L0_attn_W_qkv, L0_attn_b_qkv,
           L0_attn_W_proj, L0_attn_b_proj, L0_ffn_router_w, L0_ffn_w_in, L0_ffn_b_in, L0_ffn_w_out,
           L0_ffn_b_out):
    import numpy as np
    import concourse.bacc as bacc
    from concourse.bass_utils import run_bass_kernel_spmd

    f = lambda a: np.asarray(a)
    patches = f(x).reshape(B, 5, 16, 8, 16, 8).transpose(1, 3, 5, 0, 2, 4).reshape(320, B * N)

    def chunks(a):
        padded = np.zeros((KF * NF, a.shape[1]), a.dtype)
        padded[:320] = a
        return padded.reshape(NF, KF, -1).transpose(1, 0, 2)

    def rows(a):
        return a.reshape(NC, P, -1).transpose(1, 0, 2)

    wqkv, bqkv = f(L0_attn_W_qkv), f(L0_attn_b_qkv)
    order = lambda a: a.reshape(-1, 2, 8, 2, DH).transpose(0, 1, 3, 4, 2)
    f32 = np.float32
    arrays = {
        "xT": chunks(patches),
        "w_tok": chunks(f(L0_tok_W)),
        "w_attn": np.concatenate([rows(order(wqkv[:, :2 * D]).reshape(D, 4 * P)), rows(wqkv[:, 2 * D:]),
                                  rows(f(L0_attn_W_proj)), rows(f(L0_ffn_router_w))], 2).reshape(P, -1),
        "w_in": f(L0_ffn_w_in).reshape(E, NC, P, D).transpose(2, 0, 1, 3).reshape(P, -1),
        "w_out": f(L0_ffn_w_out).reshape(E, NC, P, D).transpose(2, 0, 1, 3),
        "columns": np.concatenate([
            np.eye(P, dtype=f32), np.tile(np.arange(E, dtype=f32), (P, 1)),
            f(L0_attn_ln_w).reshape(NC, P).T, f(L0_attn_ln_b).reshape(NC, P).T,
            order(bqkv[None, :2 * D]).reshape(4, P).T,
            f(L0_ffn_b_in).reshape(E, NC, P).transpose(2, 0, 1).reshape(P, -1)], 1),
        "row_params": np.concatenate([f(L0_tok_gamma), bqkv[2 * D:], f(L0_attn_b_proj)]),
        "b_out": f(L0_ffn_b_out),
    }
    nc = bacc.Bacc("TRN2", target_bir_lowering=False, num_devices=1)
    ins, args = {}, []
    for name, a in arrays.items():
        ins[name + "_dram"] = np.ascontiguousarray(a)
        args.append(nc.dram_tensor(name + "_dram", a.shape, mybir.dt.from_np(a.dtype), kind="ExternalInput").ap())
    args.append(nc.dram_tensor("out_dram", (B, N, D), F32, kind="ExternalOutput").ap())
    build(nc, *args)
    r = run_bass_kernel_spmd(nc, [ins], core_ids=[0])
    return r.results[0]["out_dram"]
```

```python
from contextlib import ExitStack

import concourse.bass as bass
from concourse import mybir

F32 = mybir.dt.float32
F32R = mybir.dt.float32r
BF16 = mybir.dt.bfloat16
U32 = mybir.dt.uint32
ALU = mybir.AluOpType
ACT = mybir.ActivationFunctionType
AX = mybir.AxisListType.X

P = 128
B, N, D, H, DH, E = 4, 256, 256, 16, 16, 8
NT = N // P
NC = D // P
KF = 107
NF = 3
EPS = 1e-5
SCALE = DH ** -0.5
Q_PIECE = [0, 0, 1, 1, 0, 2]
K_PIECE = [0, 1, 0, 1, 2, 0]
SLOTS = len(Q_PIECE)
MROW = SLOTS * DH
KSC = MROW + 3
BY_SWDGE = ((1, 0), (1, 2), (1, 5))
G = 4


def build(nc, xT, w_tok, w_attn, w_in, w_out, columns, row_params, b_out, out):
    with ExitStack() as ctx:
        def sb(name, shape, dt=F32):
            return ctx.enter_context(nc.sbuf_tensor(name, shape, dt))

        def sem(name):
            return ctx.enter_context(nc.semaphore(name))

        bank = [ctx.enter_context(nc.psum_tensor(f"bank{i}", [P, 512], F32)) for i in range(8)]
        ps_s, ps_t, ps_l1 = bank[0:2], bank[2:4], bank[4:6]
        ps_l2, ps_x = bank[6], bank[7]

        cols = sb("cols", [P, P + E + 2 * NC + 4 + E * NC])
        at = [0]

        def columns_of(n):
            at[0] += n
            return cols[:, at[0] - n:at[0]]

        ident, iota, lnw, lnb, bqk = (columns_of(n) for n in (P, E, NC, NC, 4))
        bin_ = columns_of(E * NC).rearrange("p (e c) -> p e c", c=NC)
        rowp = sb("rowp", [P, 3 * D])
        gam, bv, bp = (rowp[:, i * D:(i + 1) * D] for i in range(3))
        bo = sb("bo", [E, D])
        ident_b = sb("ident_b", [P, P], BF16)
        nhalf = sb("nhalf", [P, NT])
        warm = sb("warm", [P, 1])
        wt_hi, wt_lo = sb("wt_hi", [KF, NF, D], F32R), sb("wt_lo", [KF, NF, D], F32R)
        stage_a = sb("stage_a", [P, NC * (4 * P + 2 * D + E)])
        wa_raw = stage_a[:].rearrange("p (c n) -> p c n", c=NC)
        qk = stage_a[:, 0:4 * N].rearrange("p (m n) -> p m n", m=4)
        qk_r = stage_a[:, 4 * N:8 * N].rearrange("p (m n) -> p m n", m=4)
        wa_hi = sb("wa_hi", [P, NC, 4 * P + D + D + P], F32R)
        wa_lo = sb("wa_lo", [P, NC, 4 * P + D + D + P], F32R)
        OV, OP, OR = 4 * P, 4 * P + D, 4 * P + 2 * D
        stage_i = sb("stage_i", [P, E * NC * D])
        wi_raw = stage_i[:].rearrange("p (e c n) -> p e c n", e=E, c=NC)
        probs = stage_i[:].rearrange("p (h t n) -> p h t n", h=2 * G, t=NT)
        wi_hi = sb("wi_hi", [P, E, NC, D], F32R)
        wi_lo = sb("wi_lo", [P, E, NC, D], F32R)
        wo_hi = sb("wo_hi", [P, E, NC, D], F32R)
        wo_lo = sb("wo_lo", [P, E, NC, D], F32R)
        stage_o = sb("stage_o", [P, E * NC * D])
        wo_raw = stage_o[:].rearrange("p (e c n) -> p e c n", e=E, c=NC)
        wt_raw = stage_o[0:KF, 0:NF * D].rearrange("p (f n) -> p f n", f=NF)
        used = [0]

        def part(a):
            used[0] += a * D
            return stage_o[:, used[0] - a * D:used[0]].rearrange("p (a n) -> p a n", a=a)

        oT, weighted = part(G), part(NT)
        acc, g = [part(NT), part(NT)], [part(NC), part(NC)]
        lgT, gateT = part(1)[0:E, 0, :], part(1)[0:E, 0, :]
        o_n = oT[:, 0:NT, :]

        x_raw = sb("x_raw", [KF, NF, N])
        x_hi = sb("x_hi", [KF, NF, N], F32R)
        x_lo = sb("x_lo", [KF, NF, N], F32R)
        stats = sb("stats", [P, NT, 6])
        mv = sb("mv", [P, NT, 2])
        var_eps = sb("var_eps", [P, NT])
        rstd = sb("rstd", [P, NT])
        h0 = sb("h0", [P, NT, D])
        z = sb("z", [P, NT, D])
        zn = sb("zn", [P, NT, D])
        x2 = zn
        resid = [sb(f"resid{i}", [P, NT, D]) for i in range(2)]
        znT = sb("znT", [P, NC, N])
        znT_hi, znT_lo = sb("znT_hi", [P, NC, N], F32R), sb("znT_lo", [P, NC, N], F32R)
        piece = [sb(f"piece{i}", [P, 4, N], BF16) for i in range(3)]
        q_st = sb("q_st", [P, H, N], BF16)
        k_st = sb("k_st", [P, H, N], BF16)
        v_aug = sb("v_aug", [P, NT, H, 2 * DH])
        neg_max = sb("neg_max", [P, NT, H])
        m_piece = [sb(f"m_piece{i}", [P, NT, 3, H // 2], BF16) for i in range(2)]
        m_rem = sb("m_rem", [P, NT, H // 2])
        m_row = sb("m_row", [3 * H // 2, N], BF16)
        o_rs = sb("o_rs", [P, NT, H])
        oT_hi, oT_lo = sb("oT_hi", [P, NC, N], F32R), sb("oT_lo", [P, NC, N], F32R)
        x2T_hi, x2T_lo = ([sb(f"x2T_{n}{i}", [P, NC, N], F32R) for i in range(2)] for n in ("hi", "lo"))
        lg_max = sb("lg_max", [P, NT])
        ex = sb("ex", [P, NT, E])
        ex_sum = sb("ex_sum", [P, NT])
        ex_rs = sb("ex_rs", [P, NT])
        pr = sb("pr", [P, NT, E])
        top_p = sb("top_p", [P, NT, 8])
        top_i = sb("top_i", [P, NT, 8], U32)
        top_f = sb("top_f", [P, NT, 8])
        gate_a, gate_b = sb("gate_a", [P, NT, E]), sb("gate_b", [P, NT, E])
        gate = [sb(f"gate{i}", [P, NT, E]) for i in range(2)]
        g_hi, g_lo = ([sb(f"g_{n}{i}", [P, NC, N], F32R) for i in range(2)] for n in ("hi", "lo"))

        d_x = sem("d_x")
        d_wt, d_wa, d_wi, d_wo, d_out = sem("d_wt"), sem("d_wa"), sem("d_wi"), sem("d_wo"), sem("d_out")
        d_cols, d_rowp, d_bo = sem("d_cols"), sem("d_rowp"), sem("d_bo")
        d_stack, d_stack_pool = sem("d_stack"), sem("d_stack_pool")
        d_m = [sem(f"d_m{i}") for i in range(2)]
        dve_own, s_xlo, s_wt, s_wa = sem("dve_own"), sem("s_xlo"), sem("s_wt"), sem("s_wa")
        s_half = sem("s_half")
        s_mv, s_zn, s_vaug, s_max, s_mp, s_h1 = sem("s_mv"), sem("s_zn"), sem("s_vaug"), sem("s_max"), sem("s_mp"), sem("s_h1")
        s_resid, s_on, s_otlo, s_x2, s_x2lo = sem("s_resid"), sem("s_on"), sem("s_otlo"), sem("s_x2"), sem("s_x2lo")
        s_lgmax, s_gate, s_gateT, s_accini, s_acc = sem("s_lgmax"), sem("s_gate"), sem("s_gateT"), sem("s_accini"), sem("s_acc")
        s_znhi, s_znlo = sem("s_znhi"), sem("s_znlo")
        s_tok, s_znTp, s_qkp, s_vp = sem("s_tok"), sem("s_znTp"), sem("s_qkp"), sem("s_vp")
        s_S, s_mT, s_ST, s_pv = sem("s_S"), sem("s_mT"), sem("s_ST"), sem("s_pv")
        s_oTp, s_onTp, s_proj, s_x2Tp = sem("s_oTp"), sem("s_onTp"), sem("s_proj"), sem("s_x2Tp")
        s_lgTp, s_lgp, s_gTp, s_bo = sem("s_lgTp"), sem("s_lgp"), sem("s_gTp"), sem("s_bo")
        s_l1, s_l2 = sem("s_l1"), sem("s_l2")
        s_wahi, s_wihi, s_wohi = sem("s_wahi"), sem("s_wihi"), sem("s_wohi")
        s_znT, s_p0, s_qkf, s_exp = sem("s_znT"), sem("s_p0"), sem("s_qkf"), sem("s_exp")
        s_oT, s_othi, s_x2hi, s_lgT, s_ex = sem("s_oT"), sem("s_othi"), sem("s_x2hi"), sem("s_lgT"), sem("s_ex")
        s_mrow, s_identb, s_warm = sem("s_mrow"), sem("s_identb"), sem("s_warm")
        s_gelu, s_ghi, s_weighted = sem("s_gelu"), sem("s_ghi"), sem("s_weighted")
        pool_own, s_ones, s_nhalf, s_rstd = sem("pool_own"), sem("s_ones"), sem("s_nhalf"), sem("s_rstd")
        s_wilo, s_wolo, s_glo = sem("s_wilo"), sem("s_wolo"), sem("s_glo")
        s_rem, s_p1, s_p2 = ([sem(f"s_{n}{i}") for i in range(2)] for n in ("rem", "p1_", "p2_"))

        def stacked(images):
            return 16 * (2 * SLOTS * images - len(BY_SWDGE))

        out_v = out.rearrange("b (t p) d -> b p t d", p=P)

        def half(bk, i):
            return bk[:, i * N:(i + 1) * N]

        def both(bk):
            return bk[:, :].rearrange("p (t n) -> p t n", n=N)

        def two(i):
            return slice(2 * i, 2 * i + 2)

        def ps_tok(b):
            return ps_l2 if b == 1 else ps_x

        def ps_qk(b, i):
            return {(0, 1): ps_l1[0], (1, 0): ps_l2}.get((b, i), ps_x)

        def ps_v(b):
            return {0: ps_l1[1], 1: ps_l2}.get(b, ps_x)

        def ps_pv(b, i):
            return (ps_s if b else ps_l1)[i]

        def ps_expert(b, e):
            return ps_x if b == B - 1 and e % 2 else ps_l2

        def slot(st, s):
            return st[s * DH:(s + 1) * DH, :, :].rearrange("d (h m) n -> d h (m n)", m=2)

        block = ctx.enter_context(nc.Block())

        @block.sync
        def _(sp):
            def load_x(b):
                if b >= 1:
                    sp.wait_ge(s_xlo, b)
                sp.dma_start(x_raw[:], xT[:, :, b * N:(b + 1) * N]).then_inc(d_x, 16)

            def stack(b):
                if b >= 1:
                    sp.wait_ge(s_ST, H * b)
                for i, (st, table) in enumerate(((q_st, Q_PIECE), (k_st, K_PIECE))):
                    for pc in range(3):
                        if pc == 0:
                            sp.wait_ge(s_p0, 2 * b + i + 1)
                        else:
                            sp.wait_ge((s_p1, s_p2)[pc - 1][i], b + 1)
                        for s in range(SLOTS):
                            if table[s] == pc and not (b == 0 and (i, s) in BY_SWDGE):
                                sp.dma_start(slot(st, s), piece[pc][:, two(i), :]).then_inc(d_stack, 16)

            def max_rows(b, hh):
                sp.wait_ge(s_mrow, 2 * b + hh + 1)
                sp.dma_start(q_st[MROW:KSC, hh * 8:hh * 8 + 8, :], m_row[:]).then_inc(d_m[hh], 16)

            sp.dma_start(wt_raw, w_tok).then_inc(d_wt, 16)
            load_x(0)
            sp.dma_start(stage_a[:], w_attn).then_inc(d_wa, 16)
            sp.dma_start(stage_i[:], w_in).then_inc(d_wi, 16)
            load_x(1)
            sp.wait_ge(s_wt, 1)
            sp.dma_start(wo_raw, w_out).then_inc(d_wo, 16)
            load_x(2)
            stack(0)
            for t in range(B + 1):
                if t < B:
                    for hh in range(2):
                        max_rows(t, hh)
                if t + 1 < B:
                    stack(t + 1)
                if t + 3 < B:
                    load_x(t + 3)
                if t >= 1:
                    sp.wait_ge(s_acc, E * t)
                    sp.dma_start(out_v[t - 1], acc[(t - 1) % 2][:]).then_inc(d_out, 16)
            sp.wait_ge(d_out, 16 * B)

        @block.gpsimd
        def _(pool):
            n_own = [0]

            def link(ins):
                n_own[0] += 1
                ins.then_inc(pool_own, 1)
                pool.wait_ge(pool_own, n_own[0])

            def rsqrt(k):
                pool.wait_ge(s_mv, k + 1)
                link(pool.tensor_scalar(var_eps[:], mv[:, :, 1], EPS, None, ALU.add))
                pool.tensor_tensor(rstd[:], var_eps[:], nhalf[:], ALU.pow).then_inc(s_rstd, 1)

            def g_low(b, e):
                k = E * b + e
                pool.wait_ge(s_gelu, k + 1)
                pool.wait_ge(s_ghi, k + 1)
                if k >= 2:
                    pool.wait_ge(s_l2, k - 1)
                pool.tensor_tensor(g_lo[e % 2][:], g[e % 2][:], g_hi[e % 2][:].bitcast(F32), ALU.subtract).then_inc(s_glo, 1)

            def add_weighted(b, e):
                n_weighted[0] += 1
                pool.wait_ge(s_weighted, n_weighted[0])
                if e == 0:
                    pool.wait_ge(s_accini, b + 1)
                else:
                    pool.wait_ge(s_acc, E * b + e)
                pool.tensor_tensor(acc[b % 2][:], weighted[:], acc[b % 2][:], ALU.add).then_inc(s_acc, 1)

            def wi_low(experts, last=False):
                ins = pool.tensor_tensor(wi_lo[:, experts], wi_raw[:, experts], wi_hi[:, experts].bitcast(F32), ALU.subtract)
                if last:
                    ins.then_inc(s_wilo, 1)

            def wo_low():
                pool.tensor_tensor(wo_lo[:], wo_raw, wo_hi[:].bitcast(F32), ALU.subtract).then_inc(s_wolo, 1)

            n_weighted = [0]
            pool.memset(nhalf[:], -0.5).then_inc(s_nhalf, 1)
            pool.wait_ge(s_nhalf, 1)
            pool.memset(v_aug[:, :, :, DH:2 * DH], 1.0).then_inc(s_ones, 1)
            pool.wait_ge(s_ones, 1)
            pool.memset(k_st[MROW:KSC, :, :], 1.0).then_inc(s_ones, 1)
            pool.wait_ge(s_ones, 2)
            for i in range(3):
                rsqrt(ln_index(0, i))
            pool.wait_ge(s_wihi, 1)
            wi_low(slice(0, 4))
            rsqrt(ln_index(1, 0))
            for i, s in BY_SWDGE:
                pc = (Q_PIECE, K_PIECE)[i][s]
                if pc == 0:
                    pool.wait_ge(s_p0, i + 1)
                else:
                    pool.wait_ge((s_p1, s_p2)[pc - 1][i], 1)
                pool.dma_start(slot((q_st, k_st)[i], s), piece[pc][:, two(i), :]).then_inc(d_stack_pool, 16)
            rsqrt(ln_index(1, 1))
            rsqrt(ln_index(1, 2))
            wi_low(slice(4, E), last=True)
            pool.wait_ge(s_wohi, 1)
            wo_low()
            for t in range(B + 1):
                now, front, moe = t < B, 1 <= t < B - 1, t >= 1
                if moe:
                    g_low(t - 1, 0)
                if t >= 2:
                    add_weighted(t - 2, 7)
                if moe:
                    g_low(t - 1, 1)
                    add_weighted(t - 1, 0)
                    g_low(t - 1, 2)
                    add_weighted(t - 1, 1)
                    g_low(t - 1, 3)
                if front:
                    for i in range(3):
                        rsqrt(ln_index(t + 1, i))
                if moe:
                    g_low(t - 1, 4)
                    g_low(t - 1, 5)
                if now:
                    rsqrt(ln_index(t, 3))
                if moe:
                    g_low(t - 1, 6)
                    g_low(t - 1, 7)

        @block.scalar
        def _(act):
            act.dma_start(cols[:], columns).then_inc(d_cols, 16)
            act.dma_start(rowp[:], row_params.partition_broadcast(P)).then_inc(d_rowp, 16)
            act.dma_start(bo[:], b_out).then_inc(d_bo, 16)

            def znT_out(b):
                act.wait_ge(s_znTp, b + 1)
                if b == 0:
                    act.wait_ge(d_cols, 16)
                if b >= 1:
                    act.wait_ge(s_znlo, b)
                    act.wait_ge(s_znhi, b)
                act.activation(znT[:, 0, :], half(ps_tok(b), 0), ACT.Identity, bias=lnb[:, 0:1], scale=lnw[:, 0:1])
                act.activation(znT[:, 1, :], half(ps_tok(b), 1), ACT.Identity, bias=lnb[:, 1:2],
                               scale=lnw[:, 1:2]).then_inc(s_znT, 1)

            def qk_out(b, i):
                act.wait_ge(s_qkp, 2 * b + i + 1)
                if b >= 1:
                    act.wait_ge(d_stack, stacked(b))
                    act.wait_ge(s_rem[i], b)
                for m in range(2):
                    last = act.activation(piece[0][:, 2 * i + m, :], half(ps_qk(b, i), m), ACT.Identity,
                                          bias=bqk[:, 2 * i + m:2 * i + m + 1])
                last.then_inc(s_p0, 1)
                for m in range(2):
                    last = act.activation(qk[:, 2 * i + m, :], half(ps_qk(b, i), m), ACT.Identity,
                                          bias=bqk[:, 2 * i + m:2 * i + m + 1])
                last.then_inc(s_qkf, 1)

            n_warm = [0]

            def load_table(func):
                if n_warm[0]:
                    act.wait_ge(s_warm, n_warm[0])
                else:
                    act.wait_ge(s_nhalf, 1)
                n_warm[0] += 1
                act.activation(warm[:], nhalf[:, 0:1], func).then_inc(s_warm, 1)

            def max_rows_out(b, hh):
                k = 2 * b + hh
                act.wait_ge(s_mT, k + 1)
                if k >= 1:
                    act.wait_ge(d_m[(k - 1) % 2], 16 * ((k - 1) // 2 + 1))
                act.activation(m_row[:], ps_x[0:3 * H // 2, 0:N], ACT.Copy).then_inc(s_mrow, 1)

            def exp(b, h):
                act.wait_ge(s_ST, H * b + h + 1)
                if b == 0 and h == 0:
                    act.wait_ge(s_wilo, 1)
                if H * b + h >= 2 * G:
                    act.wait_ge(s_pv, (H * b + h - 2 * G) // G + 1)
                act.activation(probs[:, h % (2 * G), :, :], both(ps_t[h % 2]), ACT.Exp, scale=SCALE).then_inc(s_exp, 1)

            def o_out(b):
                act.wait_ge(s_pv, G * (b + 1))
                if b == 0:
                    act.wait_ge(s_wolo, 1)
                if b >= 1:
                    act.wait_ge(s_onTp, b)
                for i in range(2):
                    last = act.activation(oT[:, 2 * i:2 * i + 2, :], both(ps_pv(b, i)), ACT.Copy)
                last.then_inc(s_oT, 1)

            def oT_high(b):
                act.wait_ge(s_onTp, b + 1)
                if b >= 1:
                    act.wait_ge(s_proj, b)
                act.activation(oT_hi[:], both(ps_s[0]), ACT.Copy).then_inc(s_othi, 1)

            def x2T_high(b):
                act.wait_ge(s_x2Tp, b + 1)
                if b >= 2:
                    act.wait_ge(s_l1, E * (b - 1))
                act.activation(x2T_hi[b % 2][:], both(ps_t[0]), ACT.Copy).then_inc(s_x2hi, 1)

            def logits(b):
                act.wait_ge(s_lgTp, b + 1)
                if b >= 1:
                    act.wait_ge(s_lgp, b)
                act.activation(lgT, ps_t[1][0:E, 0:N], ACT.Copy).then_inc(s_lgT, 1)

            def logits_exp(b):
                act.wait_ge(s_lgmax, b + 1)
                for tt in range(NT):
                    last = act.activation(ex[:, tt, :], ps_t[0][:, tt * E:(tt + 1) * E], ACT.Exp, bias=lg_max[:, tt:tt + 1])
                last.then_inc(s_ex, 1)

            def gelu(b, e):
                k = E * b + e
                act.wait_ge(s_l1, k + 1)
                if k >= 2:
                    act.wait_ge(s_glo, k - 1)
                for hc in range(NC):
                    last = act.activation(g[e % 2][:, hc, :], half(ps_l1[e % 2], hc), ACT.Gelu_apprx_tanh,
                                          bias=bin_[:, e, hc:hc + 1])
                last.then_inc(s_gelu, 1)
                act.wait_ge(s_gelu, k + 1)
                if k >= 2:
                    act.wait_ge(s_l2, k - 1)
                act.activation(g_hi[e % 2][:], g[e % 2][:], ACT.Copy).then_inc(s_ghi, 1)

            def weigh(b, e):
                act.wait_ge(s_l2, E * b + e + 1)
                if e == 0:
                    act.wait_ge(s_gate, b + 1)
                if b > 0 or e > 0:
                    act.wait_ge(s_acc, E * b + e)
                for tt in range(NT):
                    last = act.activation(weighted[:, tt, :], half(ps_expert(b, e), tt), ACT.Copy,
                                          scale=gate[b % 2][:, tt, e:e + 1])
                last.then_inc(s_weighted, 1)

            act.wait_ge(d_wa, 16)
            act.activation(wa_hi[:, :, 0:OR + E], wa_raw, ACT.Copy).then_inc(s_wahi, 1)
            act.wait_ge(d_wi, 16)
            act.activation(wi_hi[:], wi_raw, ACT.Copy).then_inc(s_wihi, 1)
            act.wait_ge(d_cols, 16)
            act.activation(ident_b[:], ident, ACT.Copy).then_inc(s_identb, 1)
            znT_out(0)
            act.wait_ge(d_wo, 16)
            act.activation(wo_hi[:], wo_raw, ACT.Copy).then_inc(s_wohi, 1)
            qk_out(0, 0)
            qk_out(0, 1)
            for t in range(B + 1):
                now, front, moe = t < B, 1 <= t < B - 1, t >= 1
                if t == 0:
                    znT_out(1)
                if moe:
                    gelu(t - 1, 0)
                if t >= 2:
                    weigh(t - 2, 7)
                if moe:
                    gelu(t - 1, 1)
                    weigh(t - 1, 0)
                if now:
                    max_rows_out(t, 0)
                if moe:
                    gelu(t - 1, 2)
                    weigh(t - 1, 1)
                    gelu(t - 1, 3)
                if moe and now:
                    load_table(ACT.Exp)
                if now:
                    for h in range(H):
                        exp(t, h)
                        if h == (1 if t else 3):
                            max_rows_out(t, 1)
                if moe and now:
                    load_table(ACT.Gelu_apprx_tanh)
                if now:
                    o_out(t)
                if moe:
                    gelu(t - 1, 4)
                if front:
                    znT_out(t + 1)
                if now:
                    oT_high(t)
                if moe:
                    gelu(t - 1, 5)
                if front:
                    qk_out(t + 1, 0)
                if moe:
                    gelu(t - 1, 6)
                if front:
                    qk_out(t + 1, 1)
                if now:
                    x2T_high(t)
                if moe:
                    gelu(t - 1, 7)
                if moe and now:
                    load_table(ACT.Exp)
                if now:
                    logits(t)
                    logits_exp(t)
                    load_table(ACT.Gelu_apprx_tanh)

        @block.vector
        def _(dve):
            n_own = [0]

            def link(ins):
                n_own[0] += 1
                ins.then_inc(dve_own, 1)
                dve.wait_ge(dve_own, n_own[0])

            def moments(src, k, meanwhile=None):
                for tt in range(NT):
                    ins = dve.bn_stats(stats[:, tt, :], src[:, tt, :])
                link(ins)
                if k >= 1:
                    dve.wait_ge(s_rstd, k)
                for tt in range(NT):
                    ins = dve.bn_aggr(mv[:, tt, :], stats[:, tt, :])
                ins.then_inc(s_mv, 1)
                if meanwhile:
                    meanwhile()
                dve.wait_ge(s_rstd, k + 1)

            def normed(dst, src):
                for tt in range(NT):
                    ins = dve.tensor_scalar(dst[:, tt, :], src[:, tt, :], mv[:, tt, 0:1], rstd[:, tt:tt + 1],
                                            ALU.subtract, ALU.mult)
                return ins

            def split_x(b):
                dve.wait_ge(d_x, 16 * (b + 1))
                if b >= 1:
                    dve.wait_ge(s_tok, b)
                link(dve.tensor_copy(x_hi[:], x_raw[:]))
                dve.tensor_tensor(x_lo[:], x_raw[:], x_hi[:].bitcast(F32), ALU.subtract).then_inc(s_xlo, 1)

            def wa_low(cols_, chunk):
                dve.wait_ge(s_wahi, 1)
                dve.tensor_tensor(wa_lo[:, chunk, cols_], wa_raw[:, chunk, cols_], wa_hi[:, chunk, cols_].bitcast(F32),
                                  ALU.subtract).then_inc(s_wa, 1)

            def first_norm(b, meanwhile=None):
                dve.wait_ge(s_tok, b + 1)
                tok = both(ps_tok(b))
                moments(tok, ln_index(b, 0), meanwhile)
                link(normed(z, tok))
                if b == 0:
                    dve.wait_ge(d_rowp, 16)
                for tt in range(NT):
                    ins = dve.tensor_tensor(h0[:, tt, :], z[:, tt, :], gam, ALU.mult)
                link(ins)

            def later_norms(b, meanwhile=(None, None)):
                moments(h0, ln_index(b, 1), meanwhile[0])
                link(normed(z, h0))
                moments(z, ln_index(b, 2), meanwhile[1])
                if b >= 1:
                    dve.wait_ge(s_znTp, b)
                if b >= 2:
                    dve.wait_ge(s_x2Tp, b - 1)
                normed(zn, z).then_inc(s_zn, 1)

            def residual(b):
                dve.wait_ge(s_zn, b + 1)
                link(dve.tensor_tensor(z[:], z[:], h0[:], ALU.add))
                for tt in range(NT):
                    ins = dve.tensor_tensor(resid[b % 2][:, tt, :], z[:, tt, :], bp, ALU.add)
                ins.then_inc(s_resid, 1)
                dve.wait_ge(s_resid, b + 1)

            def zn_split(b):
                dve.wait_ge(s_znT, b + 1)
                if b >= 1:
                    dve.wait_ge(s_vp, b)
                dve.tensor_copy(znT_hi[:], znT[:]).then_inc(s_znhi, 1)
                dve.wait_ge(s_znhi, b + 1)
                dve.tensor_tensor(znT_lo[:], znT[:], znT_hi[:].bitcast(F32), ALU.subtract).then_inc(s_znlo, 1)

            def pieces(b, i):
                dve.wait_ge(s_p0, 2 * b + i + 1)
                dve.wait_ge(s_qkf, 2 * b + i + 1)
                if b >= 1:
                    dve.wait_ge(s_p2[i], b)
                dve.tensor_tensor(qk_r[:, two(i), :], qk[:, two(i), :], piece[0][:, two(i), :],
                                  ALU.subtract).then_inc(s_rem[i], 1)
                dve.wait_ge(s_rem[i], b + 1)
                if b >= 1:
                    dve.wait_ge(d_stack, stacked(b))
                dve.tensor_copy(piece[1][:, two(i), :], qk_r[:, two(i), :]).then_inc(s_p1[i], 1)
                dve.wait_ge(s_p1[i], b + 1)
                dve.tensor_tensor(piece[2][:, two(i), :], qk_r[:, two(i), :], piece[1][:, two(i), :],
                                  ALU.subtract).then_inc(s_p2[i], 1)

            def second_qk_out(i):
                dve.wait_ge(s_qkp, 2 + i + 1)
                dve.wait_ge(d_stack, stacked(1))
                for dst, done in ((piece[0], s_p0), (qk, s_qkf)):
                    for m in range(2):
                        ins = dve.tensor_scalar(dst[:, 2 * i + m, :], half(ps_qk(1, i), m),
                                                bqk[:, 2 * i + m:2 * i + m + 1], None, ALU.add)
                    ins.then_inc(done, 1)

            def v_out(b):
                dve.wait_ge(s_vp, b + 1)
                if b == 0:
                    dve.wait_ge(s_ones, 2)
                    dve.wait_ge(d_rowp, 16)
                if b >= 1:
                    dve.wait_ge(s_pv, G * b)
                for tt in range(NT):
                    ins = dve.tensor_tensor(v_aug[:, tt, :, 0:DH],
                                            half(ps_v(b), tt).rearrange("p (h d) -> p h d", d=DH),
                                            bv.rearrange("p (h d) -> p h d", d=DH), ALU.add)
                ins.then_inc(s_vaug, 1)

            def head_max(b, h):
                dve.wait_ge(s_S, H * b + h + 1)
                dve.tensor_reduce(neg_max[:, :, h], both(ps_s[h % 2]), AX, ALU.max, negate=True).then_inc(s_max, 1)

            def max_piece(b, hh, i):
                k = 2 * b + hh
                whole, pc = neg_max[:, :, 8 * hh:8 * hh + 8], m_piece[hh]
                if i == 0:
                    dve.wait_ge(s_max, H * b + 8 * hh + 8)
                    if b >= 1:
                        dve.wait_ge(s_mT, k - 1)
                    ins = dve.tensor_copy(pc[:, :, 0, :], whole)
                else:
                    dve.wait_ge(s_mp, 4 * k + i)
                if i == 1:
                    ins = dve.tensor_tensor(m_rem[:], whole, pc[:, :, 0, :], ALU.subtract)
                if i == 2:
                    ins = dve.tensor_copy(pc[:, :, 1, :], m_rem[:])
                if i == 3:
                    ins = dve.tensor_tensor(pc[:, :, 2, :], m_rem[:], pc[:, :, 1, :], ALU.subtract)
                ins.then_inc(s_mp, 1)

            def add_expert(b, e):
                k = E * b + e
                dve.wait_ge(s_l2, k + 1)
                a = acc[b % 2]
                if e == 0:
                    dve.wait_ge(s_accini, b + 1)
                else:
                    dve.wait_ge(s_acc, k)
                for tt in range(NT):
                    ins = dve.scalar_tensor_tensor(out=a[:, tt, :], in0=half(ps_expert(b, e), tt), scalar=gate[b % 2][:, tt, e:e + 1],
                                                   in1=a[:, tt, :], op0=ALU.mult, op1=ALU.add)
                ins.then_inc(s_acc, 1)

            def normalise(b):
                dve.wait_ge(s_oTp, b + 1)
                heads = [ps_t[tt][:, :].rearrange("p (h d) -> p h d", d=2 * DH) for tt in range(NT)]
                for tt in range(NT):
                    ins = dve.reciprocal(o_rs[:, tt, :], heads[tt][:, :, DH])
                link(ins)
                for tt in range(NT):
                    ins = dve.tensor_tensor(o_n[:, tt, :].rearrange("p (h d) -> p h d", d=DH), heads[tt][:, :, 0:DH],
                                            o_rs[:, tt, :].unsqueeze(2).to_broadcast([P, H, DH]), ALU.mult)
                ins.then_inc(s_on, 1)

            def oT_low(b):
                dve.wait_ge(s_othi, b + 1)
                dve.tensor_tensor(oT_lo[:], both(ps_s[0]), oT_hi[:].bitcast(F32), ALU.subtract).then_inc(s_otlo, 1)

            def attn_out(b, meanwhile):
                h1 = acc[b % 2]
                dve.wait_ge(s_proj, b + 1)
                if b >= 2:
                    dve.wait_ge(d_out, 16 * (b - 1))
                dve.tensor_tensor(h1[:], both(ps_s[1]), resid[b % 2][:], ALU.add).then_inc(s_h1, 1)
                dve.wait_ge(s_h1, b + 1)
                moments(h1, ln_index(b, 3), meanwhile)
                dve.wait_ge(s_znTp, min(b + 2, B))
                if b >= 1:
                    dve.wait_ge(s_x2Tp, b)
                normed(x2, h1).then_inc(s_x2, 1)

            def x2T_low(b):
                dve.wait_ge(s_x2hi, b + 1)
                dve.tensor_tensor(x2T_lo[b % 2][:], both(ps_t[0]), x2T_hi[b % 2][:].bitcast(F32),
                                  ALU.subtract).then_inc(s_x2lo, 1)

            def logits_max(b):
                dve.wait_ge(s_lgp, b + 1)
                lg = ps_t[0][:, 0:NT * E].rearrange("p (t e) -> p t e", e=E)
                dve.tensor_reduce(lg_max[:], lg, AX, ALU.max, negate=True).then_inc(s_lgmax, 1)

            def gates(b):
                dve.wait_ge(s_ex, b + 1)
                link(dve.tensor_reduce(ex_sum[:], ex[:], AX, ALU.add))
                link(dve.reciprocal(ex_rs[:], ex_sum[:]))
                link(dve.tensor_tensor(pr[:], ex[:], ex_rs[:].unsqueeze(2).to_broadcast([P, NT, E]), ALU.mult))
                for tt in range(NT):
                    ins = dve.max(top_p[:, tt, :], pr[:, tt, :])
                link(ins)
                for tt in range(NT):
                    ins = dve.max_index(top_i[:, tt, :], top_p[:, tt, :], pr[:, tt, :])
                link(ins)
                link(dve.tensor_copy(top_f[:], top_i[:]))
                if b == 0:
                    dve.wait_ge(d_cols, 16)
                for tt in range(NT):
                    for i, dst in enumerate((gate_a, gate_b)):
                        ins = dve.tensor_scalar(dst[:, tt, :], iota, top_f[:, tt, i:i + 1], top_p[:, tt, i:i + 1],
                                                ALU.is_equal, ALU.mult)
                link(ins)
                dve.tensor_tensor(gate[b % 2][:], gate_a[:], gate_b[:], ALU.add).then_inc(s_gate, 1)

            def gates_transposed(b):
                dve.wait_ge(s_gTp, b + 1)
                dve.tensor_copy(gateT, ps_t[1][0:E, 0:N]).then_inc(s_gateT, 1)

            def first_acc(b):
                dve.wait_ge(s_bo, b + 1)
                dve.tensor_tensor(acc[b % 2][:], both(ps_t[0]), acc[b % 2][:], ALU.add).then_inc(s_accini, 1)

            dve.wait_ge(d_wt, 16)
            dve.tensor_copy(wt_hi[:], wt_raw[:]).then_inc(s_half, 1)
            dve.wait_ge(d_x, 16)
            dve.tensor_copy(x_hi[:], x_raw[:]).then_inc(s_half, 1)
            dve.wait_ge(s_half, 2)
            dve.tensor_tensor(wt_lo[:], wt_raw[:], wt_hi[:].bitcast(F32), ALU.subtract).then_inc(s_wt, 1)
            dve.tensor_tensor(x_lo[:], x_raw[:], x_hi[:].bitcast(F32), ALU.subtract).then_inc(s_xlo, 1)
            link(dve.memset(wa_hi[:, :, OR + E:OR + P].bitcast(F32), 0.0))
            link(dve.memset(wa_lo[:, :, OR + E:OR + P].bitcast(F32), 0.0))
            first_norm(0, lambda: wa_low(slice(0, OV), slice(0, 1)))
            later_norms(0, (lambda: wa_low(slice(0, OV), slice(1, 2)), lambda: split_x(1)))
            residual(0)
            wa_low(slice(OV, OR + E), slice(0, NC))
            zn_split(0)
            first_norm(1)
            pieces(0, 0)
            pieces(0, 1)
            v_out(0)
            later_norms(1, (None, lambda: (head_max(0, 0), head_max(0, 1))))
            for t in range(B + 1):
                now, front, moe = t < B, 1 <= t < B - 1, t >= 1
                def heads(h, t=t):
                    if t == 1:
                        h = h + 8 if h < 8 else H
                    if t < B and h < H:
                        head_max(t, h)
                        head_max(t, h + 1)

                if t == 1:
                    for i in range(4):
                        max_piece(1, 0, i)
                if t:
                    heads(0)
                heads(2)
                if moe:
                    gates_transposed(t - 1)
                heads(4)
                if moe:
                    first_acc(t - 1)
                heads(6)
                for i in range(4):
                    if now and t != 1:
                        max_piece(t, 0, i)
                    if t < B and t != 1:
                        head_max(t, 8 + i)
                heads(12)
                heads(14)
                if now:
                    for i in range(4):
                        max_piece(t, 1, i)
                if moe:
                    add_expert(t - 1, 2)
                if front:
                    first_norm(t + 1)
                    later_norms(t + 1)
                    residual(t + 1)
                if t == 0:
                    zn_split(1)
                    residual(1)
                    for i in range(2):
                        second_qk_out(i)
                        pieces(1, i)
                if t + 2 < B:
                    split_x(t + 2)
                if t == 0:
                    v_out(1)
                if now:
                    normalise(t)
                if moe:
                    add_expert(t - 1, 3)
                if front:
                    zn_split(t + 1)
                if now:
                    oT_low(t)
                if moe:
                    add_expert(t - 1, 4)
                if now:
                    attn_out(t, (lambda b=t + 1: pieces(b, 0)) if front else (lambda: head_max(1, 0)) if t == 0 else None)
                if t == 0:
                    head_max(1, 1)
                if moe:
                    add_expert(t - 1, 5)
                if front:
                    pieces(t + 1, 1)
                if now:
                    x2T_low(t)
                if t == 0:
                    head_max(1, 2)
                    head_max(1, 3)
                if moe:
                    add_expert(t - 1, 6)
                if front:
                    v_out(t + 1)
                if now:
                    logits_max(t)
                if t == 0:
                    head_max(1, 4)
                if now:
                    gates(t)
                if t == 0:
                    for h in range(5, 8):
                        head_max(1, h)
            add_expert(B - 1, 7)

        @block.tensor
        def _(pe):
            def product(o, pairs):
                for i, (w, x) in enumerate(pairs):
                    mm = pe.matmul(o, w, x, start=(i == 0), stop=(i == len(pairs) - 1))
                return mm

            def three(w_hi, w_lo, x_hi_, x_lo_):
                return [(w_hi, x_hi_), (w_lo, x_hi_), (w_hi, x_lo_)]

            def tok(b):
                if b == 0:
                    pe.wait_ge(s_half, 2)
                else:
                    pe.wait_ge(s_xlo, b + 1)
                if b >= 2:
                    pe.wait_ge(s_mrow, 2 * b)
                for tt in range(NT):
                    c = slice(tt * P, (tt + 1) * P)
                    for i, (x, w) in enumerate(((x_hi, wt_hi), (x_hi, wt_lo), (x_lo, wt_hi))):
                        if b == 0 and tt == 0 and i == 1:
                            pe.wait_ge(s_wt, 1)
                        if b == 0 and tt == 0 and i == 2:
                            pe.wait_ge(s_xlo, 1)
                        for c3 in range(NF):
                            mm = pe.matmul(half(ps_tok(b), tt), x[:, c3, c], w[:, c3, :],
                                           start=(i + c3 == 0), stop=(i == 2 and c3 == NF - 1))
                mm.then_inc(s_tok, 1)

            def zn_transposes(b):
                pe.wait_ge(s_zn, b + 1)
                if b == 0:
                    pe.wait_ge(d_cols, 16)
                for c in range(NC):
                    for tt in range(NT):
                        mm = pe.transpose(ps_tok(b)[:, c * N + tt * P:c * N + (tt + 1) * P],
                                          zn[:, tt, c * P:(c + 1) * P], ident)
                mm.then_inc(s_znTp, 1)

            def qk_product(b, i):
                if i == 0:
                    pe.wait_ge(s_znhi, b + 1)
                    pe.wait_ge(s_znlo, b + 1)
                    if b == 0:
                        pe.wait_ge(s_wa, 2)
                elif b == 1:
                    pe.wait_ge(s_mrow, 2)
                elif b >= 2:
                    pe.wait_ge(s_qkf, 2 * b + 1)
                for m in range(2):
                    cs = slice((2 * i + m) * P, (2 * i + m + 1) * P)
                    mm = product(half(ps_qk(b, i), m), [
                        pr for c in range(NC)
                        for pr in three(wa_hi[:, c, cs], wa_lo[:, c, cs], znT_hi[:, c, :], znT_lo[:, c, :])])
                mm.then_inc(s_qkp, 1)

            def v_product(b):
                if b == 0:
                    pe.wait_ge(s_wa, 3)
                if b == 1:
                    pe.wait_ge(s_qkf, 3)
                if b >= 2:
                    pe.wait_ge(s_qkf, 2 * b + 2)
                for tt in range(NT):
                    t_ = slice(tt * P, (tt + 1) * P)
                    mm = product(half(ps_v(b), tt), [
                        pr for c in range(NC)
                        for pr in three(znT_hi[:, c, t_], znT_lo[:, c, t_], wa_hi[:, c, OV:OP], wa_lo[:, c, OV:OP])])
                mm.then_inc(s_vp, 1)

            def scores(b, h):
                if h == 0:
                    pe.wait_ge(d_stack, stacked(b + 1))
                    if b == 0:
                        pe.wait_ge(d_stack_pool, 16 * len(BY_SWDGE))
                    if b >= 1:
                        pe.wait_ge(s_h1, b)
                if H * b + h >= 2:
                    pe.wait_ge(s_max, H * b + h - 1)
                for tt in range(NT):
                    mm = pe.matmul(half(ps_s[h % 2], tt), q_st[0:MROW, h, tt * P:(tt + 1) * P],
                                   k_st[0:MROW, h, :], start=True, stop=True)
                mm.then_inc(s_S, 1)

            def max_transposes(b, hh):
                pe.wait_ge(s_mp, 4 * (2 * b + hh + 1))
                if b + hh == 0:
                    pe.wait_ge(s_identb, 1)
                if hh == 1:
                    pe.wait_ge(s_mrow, 2 * b + 1)
                elif b < 2:
                    pe.wait_ge(s_qkf, 3 * b + 1)
                else:
                    pe.wait_ge(s_vaug, b + 1)
                for tt in range(NT):
                    mm = pe.matmul(ps_x[0:3 * H // 2, tt * P:(tt + 1) * P],
                                   m_piece[hh][:, tt, :, :].rearrange("p r h -> p (r h)"), ident_b[:],
                                   start=True, stop=True)
                mm.then_inc(s_mT, 1)

            def scores_t(b, h):
                if h % 8 == 0:
                    pe.wait_ge(d_m[h // 8], 16 * (b + 1))
                if h == 0 and b == 0:
                    pe.wait_ge(s_ones, 2)
                if h == 0 and b >= 1:
                    pe.wait_ge(s_accini, b)
                if H * b + h >= 2:
                    pe.wait_ge(s_exp, H * b + h - 1)
                for tt in range(NT):
                    mm = pe.matmul(half(ps_t[h % 2], tt), k_st[0:KSC, h, tt * P:(tt + 1) * P],
                                   q_st[0:KSC, h, :], start=True, stop=True)
                mm.then_inc(s_ST, 1)

            def pv(b, gr):
                pe.wait_ge(s_exp, H * b + G * (gr + 1))
                if gr == 0:
                    pe.wait_ge(s_vaug, b + 1)
                    if b == 0:
                        pe.wait_ge(s_qkf, 2)
                    else:
                        pe.wait_ge(s_max, H * (b + 1))
                for tt in range(NT):
                    for j in range(G):
                        h = G * gr + j
                        mm = pe.matmul(ps_pv(b, gr // 2)[32 * j:32 * j + 32, (gr % 2) * N:(gr % 2 + 1) * N],
                                       v_aug[:, tt, h, :], probs[:, h % (2 * G), tt, :],
                                       start=(tt == 0), stop=(tt == NT - 1))
                mm.then_inc(s_pv, 1)

            def o_transposes(b):
                pe.wait_ge(s_oT, b + 1)
                pe.wait_ge(s_exp, H * (b + 1))
                for tt in range(NT):
                    for gr in range(G):
                        mm = pe.transpose(ps_t[tt][:, gr * P:(gr + 1) * P], oT[:, gr, tt * P:(tt + 1) * P], ident)
                mm.then_inc(s_oTp, 1)

            def on_transposes(b):
                pe.wait_ge(s_on, b + 1)
                for c in range(NC):
                    for tt in range(NT):
                        mm = pe.transpose(ps_s[0][:, c * N + tt * P:c * N + (tt + 1) * P],
                                          o_n[:, tt, c * P:(c + 1) * P], ident)
                mm.then_inc(s_onTp, 1)

            def projection(b):
                pe.wait_ge(s_othi, b + 1)
                pe.wait_ge(s_otlo, b + 1)
                for tt in range(NT):
                    t_ = slice(tt * P, (tt + 1) * P)
                    mm = product(half(ps_s[1], tt), [
                        pr for c in range(NC)
                        for pr in three(oT_hi[:, c, t_], oT_lo[:, c, t_], wa_hi[:, c, OP:OR], wa_lo[:, c, OP:OR])])
                mm.then_inc(s_proj, 1)

            def x2_transposes(b):
                pe.wait_ge(s_x2, b + 1)
                for c in range(NC):
                    for tt in range(NT):
                        mm = pe.transpose(ps_t[0][:, c * N + tt * P:c * N + (tt + 1) * P],
                                          x2[:, tt, c * P:(c + 1) * P], ident)
                mm.then_inc(s_x2Tp, 1)

            def router(b):
                pe.wait_ge(s_x2hi, b + 1)
                pe.wait_ge(s_x2lo, b + 1)
                rt = slice(OR, OR + P)
                product(ps_t[1][:, 0:N], [
                    pr for c in range(NC)
                    for pr in three(wa_hi[:, c, rt], wa_lo[:, c, rt], x2T_hi[b % 2][:, c, :], x2T_lo[b % 2][:, c, :])
                ]).then_inc(s_lgTp, 1)

            def logits_transposes(b):
                pe.wait_ge(s_lgT, b + 1)
                for tt in range(NT):
                    mm = pe.transpose(ps_t[0][:, tt * E:(tt + 1) * E], lgT[:, tt * P:(tt + 1) * P], ident[0:E, 0:E])
                mm.then_inc(s_lgp, 1)

            def gate_transposes(b):
                pe.wait_ge(s_gate, b + 1)
                for tt in range(NT):
                    mm = pe.transpose(ps_t[1][0:E, tt * P:(tt + 1) * P], gate[b % 2][:, tt, :], ident)
                mm.then_inc(s_gTp, 1)

            def b_out_product(b):
                pe.wait_ge(s_gateT, b + 1)
                if b == 0:
                    pe.wait_ge(d_bo, 16)
                for tt in range(NT):
                    mm = pe.matmul(half(ps_t[0], tt), gateT[:, tt * P:(tt + 1) * P], bo[:], start=True, stop=True)
                mm.then_inc(s_bo, 1)

            def layer1(b, e):
                k = E * b + e
                if k == 0:
                    pe.wait_ge(s_wilo, 1)
                    pe.wait_ge(s_oT, 1)
                if k >= 2:
                    pe.wait_ge(s_gelu, k - 1)
                for hc in range(NC):
                    hs = slice(hc * P, (hc + 1) * P)
                    mm = product(half(ps_l1[e % 2], hc), [
                        pr for c in range(NC)
                        for pr in three(wi_hi[:, e, c, hs], wi_lo[:, e, c, hs],
                                        x2T_hi[b % 2][:, c, :], x2T_lo[b % 2][:, c, :])])
                mm.then_inc(s_l1, 1)

            def layer2(b, e):
                k = E * b + e
                pe.wait_ge(s_ghi, k + 1)
                if k == 0:
                    pe.wait_ge(s_wolo, 1)
                    pe.wait_ge(s_vaug, 2)
                pending = k - 2 if b == B - 1 and e >= 2 else k - 1
                if pending >= 0:
                    if pending % E in BY_POOL and not (pending // E == B - 1 and pending % E == 7):
                        pe.wait_ge(s_weighted, weighted_before(pending) + 1)
                    else:
                        pe.wait_ge(s_acc, pending + 1)
                for tt in range(NT):
                    t_ = slice(tt * P, (tt + 1) * P)
                    for i, (hc, w) in enumerate([(hc, w) for w in (wo_hi, wo_lo) for hc in range(NC)]):
                        pe.matmul(half(ps_expert(b, e), tt), g_hi[e % 2][:, hc, t_], w[:, e, hc, :], start=(i == 0), stop=False)
                    pe.wait_ge(s_glo, k + 1)
                    for hc in range(NC):
                        mm = pe.matmul(half(ps_expert(b, e), tt), g_lo[e % 2][:, hc, t_], wo_hi[:, e, hc, :],
                                       start=False, stop=(hc == NC - 1))
                mm.then_inc(s_l2, 1)

            tok(0)
            zn_transposes(0)
            tok(1)
            qk_product(0, 0)
            qk_product(0, 1)
            v_product(0)
            for t in range(B + 1):
                now, front, moe = t < B, 1 <= t < B - 1, t >= 1
                def heads(h, t=t):
                    if t == 1:
                        h = h + 8 if h < 8 else H
                    if t < B and h < H:
                        scores(t, h)
                        scores(t, h + 1)

                if t != 1:
                    heads(0)
                if t >= 2:
                    layer1(t - 1, 0)
                    layer1(t - 1, 1)
                if t == 1:
                    heads(0)
                    max_transposes(1, 0)
                    layer2(0, 0)
                heads(2)
                if t == 0:
                    zn_transposes(1)
                if t == 1:
                    layer1(0, 2)
                if moe:
                    gate_transposes(t - 1)
                heads(4)
                if moe:
                    b_out_product(t - 1)
                heads(6)
                if t >= 2:
                    layer2(t - 1, 0)
                heads(8)
                if t >= 2:
                    layer1(t - 1, 2)
                heads(10)
                if moe:
                    layer2(t - 1, 1)
                if now and t != 1:
                    max_transposes(t, 0)
                heads(12)
                if moe:
                    layer1(t - 1, 3)
                heads(14)
                if moe and not now:
                    layer2(t - 1, 2)
                if now:
                    for pair in range(H // 2):
                        scores_t(t, 2 * pair)
                        scores_t(t, 2 * pair + 1)
                        if pair == 0 and moe:
                            layer2(t - 1, 2)
                        if pair == (0 if t else 1):
                            max_transposes(t, 1)
                        if pair == 0 and moe:
                            layer1(t - 1, 4)
                        if pair == 1 and front:
                            tok(t + 1)
                        if pair in (2, 4) and t == 0:
                            qk_product(1, (2, 4).index(pair))
                        if pair == 4 and moe:
                            layer1(t - 1, 5)
                        if pair in (3, 5, 7):
                            pv(t, pair // 2 - 1)
                    pv(t, G - 1)
                    if t == 0:
                        v_product(1)
                if moe and not now:
                    layer1(t - 1, 4)
                if moe:
                    layer2(t - 1, 3)
                if moe and not now:
                    layer1(t - 1, 5)
                if now:
                    o_transposes(t)
                if front:
                    zn_transposes(t + 1)
                if moe:
                    layer1(t - 1, 6)
                if now:
                    on_transposes(t)
                if moe:
                    layer2(t - 1, 4)
                if front:
                    qk_product(t + 1, 0)
                if now:
                    projection(t)
                if moe and not now:
                    layer1(t - 1, 7)
                if moe:
                    layer2(t - 1, 5)
                if front:
                    qk_product(t + 1, 1)
                if moe and now:
                    layer1(t - 1, 7)
                if t == 0:
                    scores(1, 0)
                    scores(1, 1)
                if now:
                    x2_transposes(t)
                if t == 0:
                    scores(1, 2)
                    scores(1, 3)
                if front:
                    v_product(t + 1)
                if moe and now:
                    layer2(t - 1, 6)
                if now:
                    router(t)
                if t == 0:
                    scores(1, 4)
                if now:
                    logits_transposes(t)
                if t == 0:
                    layer1(0, 0)
                    scores(1, 5)
                    scores(1, 6)
                    layer1(0, 1)
                    scores(1, 7)
                if moe and not now:
                    layer2(t - 1, 6)
                if moe:
                    layer2(t - 1, 7)


BY_POOL = (0, 1, 7)


def weighted_before(k):
    return sum(j % E in BY_POOL for j in range(k))


def ln_index(b, i):
    if i < 3:
        return i if b == 0 else 3 + 4 * (b - 1) + i
    return 3 + 4 * b + (3 if b + 1 < B else 0)


def kernel(x, L0_tok_W, L0_tok_gamma, L0_attn_ln_w, L0_attn_ln_b, L0_attn_W_qkv, L0_attn_b_qkv,
           L0_attn_W_proj, L0_attn_b_proj, L0_ffn_router_w, L0_ffn_w_in, L0_ffn_b_in, L0_ffn_w_out,
           L0_ffn_b_out):
    import numpy as np
    import concourse.bacc as bacc
    from concourse.bass_utils import run_bass_kernel_spmd

    f = lambda a: np.asarray(a)
    patches = f(x).reshape(B, 5, 16, 8, 16, 8).transpose(1, 3, 5, 0, 2, 4).reshape(320, B * N)

    def chunks(a):
        padded = np.zeros((KF * NF, a.shape[1]), a.dtype)
        padded[:320] = a
        return padded.reshape(NF, KF, -1).transpose(1, 0, 2)

    def rows(a):
        return a.reshape(NC, P, -1).transpose(1, 0, 2)

    wqkv, bqkv = f(L0_attn_W_qkv), f(L0_attn_b_qkv)
    order = lambda a: a.reshape(-1, 2, 8, 2, DH).transpose(0, 1, 3, 4, 2)
    f32 = np.float32
    arrays = {
        "xT": chunks(patches),
        "w_tok": chunks(f(L0_tok_W)),
        "w_attn": np.concatenate([rows(order(wqkv[:, :2 * D]).reshape(D, 4 * P)), rows(wqkv[:, 2 * D:]),
                                  rows(f(L0_attn_W_proj)), rows(f(L0_ffn_router_w))], 2).reshape(P, -1),
        "w_in": f(L0_ffn_w_in).reshape(E, NC, P, D).transpose(2, 0, 1, 3).reshape(P, -1),
        "w_out": f(L0_ffn_w_out).reshape(E, NC, P, D).transpose(2, 0, 1, 3),
        "columns": np.concatenate([
            np.eye(P, dtype=f32), np.tile(np.arange(E, dtype=f32), (P, 1)),
            f(L0_attn_ln_w).reshape(NC, P).T, f(L0_attn_ln_b).reshape(NC, P).T,
            order(bqkv[None, :2 * D]).reshape(4, P).T,
            f(L0_ffn_b_in).reshape(E, NC, P).transpose(2, 0, 1).reshape(P, -1)], 1),
        "row_params": np.concatenate([f(L0_tok_gamma), bqkv[2 * D:], f(L0_attn_b_proj)]),
        "b_out": f(L0_ffn_b_out),
    }
    nc = bacc.Bacc("TRN2", target_bir_lowering=False, num_devices=1)
    ins, args = {}, []
    for name, a in arrays.items():
        ins[name + "_dram"] = np.ascontiguousarray(a)
        args.append(nc.dram_tensor(name + "_dram", a.shape, mybir.dt.from_np(a.dtype), kind="ExternalInput").ap())
    args.append(nc.dram_tensor("out_dram", (B, N, D), F32, kind="ExternalOutput").ap())
    build(nc, *args)
    r = run_bass_kernel_spmd(nc, [ins], core_ids=[0])
    return r.results[0]["out_dram"]
```
